# Optimizing a Trainium2 kernel written in Bass

```python
import numpy as np
import jax
import jax.numpy as jnp

def _softmax(x, axis=-1):
    return jax.nn.softmax(x, axis=axis)

def _gelu(x):
    return jax.nn.gelu(x, approximate=True)

def _silu(x):
    return jax.nn.silu(x)

def _sigmoid(x):
    return jax.nn.sigmoid(x)

def _layernorm(x, axis=-1, eps=1e-05):
    m = jnp.mean(x, axis=axis, keepdims=True)
    v = jnp.var(x, axis=axis, keepdims=True)
    return (x - m) / jnp.sqrt(v + eps)

def _scatter_add(tgt, idx, src, axis=0):
    return tgt.at[idx].add(src)

def _segment_sum(src, seg, n):
    return jax.ops.segment_sum(src, seg, n)
kernel_name = 'mk_audio_tower_d1_tok_audfeat512_r4_00b314'

def setup_inputs(seed: int=0):
    np.random.seed(seed)
    _w = jnp.asarray

    def _rec_inputs():
        import jax
        import jax.numpy as jnp
        _rk = jax.random.key(seed)
        x = -0.000125008 + 0.999885 * jax.random.normal(jax.random.fold_in(_rk, 1), (4, 750, 64), jnp.float32)
        return x
    x = _rec_inputs()

    def _L0_tok_setup():
        import jax, jax.numpy as jnp
        import numpy as np
        CONTEXT = 5
        STRIDE = 1
        DILATION = 1
        PADDING = 0
        key = jax.random.key(seed)
        k1, k2, k3 = jax.random.split(key, 3)
        B, T, D, O = (32, 1024, 64, 128)
        x = jax.random.normal(k1, (B, T, D), dtype=jnp.float32)
        W = jax.random.normal(k2, (O, CONTEXT * D), dtype=jnp.float32) * 0.02
        b = jax.random.normal(k3, (O,), dtype=jnp.float32) * 0.02
        return {'x': x, 'W': W, 'b': b}
    _L0_tok_all = _L0_tok_setup()
    _L0_tok_in = {k: v for k, v in _L0_tok_all.items() if k in ('W', 'b')}
    del _L0_tok_all

    def _L0_attn_setup():
        import jax, jax.numpy as jnp
        import numpy as np
        from math import sqrt
        key = jax.random.key(seed)
        k1, k2, k3, k4 = jax.random.split(key, 4)
        bs, N, D, H = (2, 1024, 128, 8)
        z = jax.random.normal(k1, (bs, N, D), dtype=jnp.float32)
        w_qkv = jax.random.normal(k2, (3 * D, D), dtype=jnp.float32) * (1.0 / sqrt(D))
        w_agg = jax.random.normal(k3, (D, D), dtype=jnp.float32) * (1.0 / sqrt(D))
        b_agg = jax.random.normal(k4, (D,), dtype=jnp.float32) * 0.01
        return {'z': z, 'w_qkv': w_qkv, 'w_agg': w_agg, 'b_agg': b_agg}
    _L0_attn_all = _L0_attn_setup()
    _L0_attn_in = {k: v for k, v in _L0_attn_all.items() if k in ('w_qkv', 'w_agg', 'b_agg')}
    del _L0_attn_all

    def _L0_ffn_setup():
        import jax, jax.numpy as jnp
        import numpy as np
        B, N, D, E = (8, 2048, 128, 8)
        H = 2 * D
        key = jax.random.key(seed)
        ks = jax.random.split(key, 7)
        s = 0.02
        return {'x': jax.random.normal(ks[0], (B, N, D), dtype=jnp.float32), 'W1': jax.random.normal(ks[1], (E, D, H), dtype=jnp.float32) * s, 'b1': jnp.zeros((E, H), dtype=jnp.float32), 'W2': jax.random.normal(ks[2], (E, H, D), dtype=jnp.float32) * s, 'b2': jnp.zeros((E, D), dtype=jnp.float32), 'Wg': jax.random.normal(ks[3], (D, E), dtype=jnp.float32) * s, 'bg': jnp.zeros((E,), dtype=jnp.float32)}
    _L0_ffn_all = _L0_ffn_setup()
    _L0_ffn_in = {k: v for k, v in _L0_ffn_all.items() if k in ('W1', 'b1', 'W2', 'b2', 'Wg', 'bg')}
    del _L0_ffn_all
    return {'x': x, 'L0_tok_W': _L0_tok_in['W'], 'L0_tok_b': _L0_tok_in['b'], 'L0_attn_w_qkv': _L0_attn_in['w_qkv'], 'L0_attn_w_agg': _L0_attn_in['w_agg'], 'L0_attn_b_agg': _L0_attn_in['b_agg'], 'L0_ffn_W1': _L0_ffn_in['W1'], 'L0_ffn_b1': _L0_ffn_in['b1'], 'L0_ffn_W2': _L0_ffn_in['W2'], 'L0_ffn_b2': _L0_ffn_in['b2'], 'L0_ffn_Wg': _L0_ffn_in['Wg'], 'L0_ffn_bg': _L0_ffn_in['bg']}

def reference(x, L0_tok_W, L0_tok_b, L0_attn_w_qkv, L0_attn_w_agg, L0_attn_b_agg, L0_ffn_W1, L0_ffn_b1, L0_ffn_W2, L0_ffn_b2, L0_ffn_Wg, L0_ffn_bg):
    import jax
    import jax.numpy as jnp

    def _L0_tok_ref(x, W, b):
        import jax, jax.numpy as jnp
        import numpy as np
        CONTEXT = 5
        STRIDE = 1
        DILATION = 1
        PADDING = 0
        'TDNN forward: unfold(context over time) + Linear == dilated 1D conv.\n\n            x: (B, T, D); W: (O, CONTEXT*D) with layout W[o, c*D + d]; b: (O,)\n            returns (B, L, O) where L = (T + 2*PADDING - DILATION*(CONTEXT-1) - 1)//STRIDE + 1\n            '
        B, T, D = x.shape
        O = W.shape[0]
        kernel = W.reshape(O, CONTEXT, D).transpose(1, 2, 0)
        out = jax.lax.conv_general_dilated(x, kernel, window_strides=(STRIDE,), padding=[(PADDING, PADDING)], rhs_dilation=(DILATION,), dimension_numbers=('NHC', 'HIO', 'NHC'))
        return out + b

    def _L0_attn_ref(z, w_qkv, w_agg, b_agg):
        import jax, jax.numpy as jnp
        import numpy as np
        from math import sqrt
        bs, N, D = z.shape
        H = 8
        Dh = D // H
        qkv = jnp.einsum('bnd,ed->bne', z, w_qkv).reshape(bs, N, 3, H, Dh)
        q, k, v = jnp.moveaxis(qkv, 2, 0)
        q = q.transpose(0, 2, 1, 3)
        k = k.transpose(0, 2, 1, 3)
        v = v.transpose(0, 2, 1, 3)
        scores = jnp.einsum('bhnd,bhmd->bhnm', q, k) / sqrt(Dh)
        attn = jax.nn.softmax(scores, axis=-1)
        sa = jnp.einsum('bhnm,bhmd->bhnd', attn, v)
        sa = sa.transpose(0, 2, 1, 3).reshape(bs, N, H * Dh)
        out = jnp.einsum('bnd,ed->bne', sa, w_agg) + b_agg
        return out

    def _L0_ffn_ref(x, W1, b1, W2, b2, Wg, bg):
        import jax, jax.numpy as jnp
        import numpy as np
        B, N, D, E = (8, 2048, 128, 8)
        H = 2 * D
        Bs, Ns, Ds = x.shape
        xf = x.reshape(Bs * Ns, Ds)
        logits = xf @ Wg + bg
        idx = jnp.argmax(logits, axis=-1)
        out = jnp.zeros_like(xf)
        num_experts = W1.shape[0]
        for e in range(num_experts):
            h = jax.nn.relu(xf @ W1[e] + b1[e])
            y = h @ W2[e] + b2[e]
            out = jnp.where((idx == e)[:, None], y, out)
        return out.reshape(Bs, Ns, Ds)
    h = _L0_tok_ref(x, L0_tok_W, L0_tok_b)
    h = h + _L0_attn_ref(_layernorm(h, axis=-1), L0_attn_w_qkv, L0_attn_w_agg, L0_attn_b_agg)
    h = h + _L0_ffn_ref(_layernorm(h, axis=-1), L0_ffn_W1, L0_ffn_b1, L0_ffn_W2, L0_ffn_b2, L0_ffn_Wg, L0_ffn_bg)
    return h

_drawn_inputs = setup_inputs


def setup_inputs(seed=0):
    import zlib

    import numpy as np

    out = dict(_drawn_inputs(seed))
    spreads = {'L0_ffn_b1': (0.0, 0.1), 'L0_ffn_b2': (0.0, 0.1), 'L0_ffn_bg': (0.0, 0.1)}
    factors = {}
    for name, (base, spread) in spreads.items():
        noise = np.random.default_rng([zlib.crc32(name.encode()), seed]).standard_normal(out[name].shape)
        drawn = base * np.exp(spread * noise) if base else spread * noise
        out[name] = jnp.asarray(drawn.astype(out[name].dtype))
    for name, factor in factors.items():
        out[name] = (out[name] * factor).astype(out[name].dtype)
    return out
```

```python
import struct
from contextlib import ExitStack

import concourse.bass as bass
from concourse import mybir


def _program(nc, x, tok_w, tok_b, w_qkv, w_agg, b_agg, w1, b1, w2, b2, wg, bg, out):
    F32, BF16 = mybir.dt.float32, mybir.dt.bfloat16
    I32, U32 = mybir.dt.int32, mybir.dt.uint32
    ALU, ACT, AX = mybir.AluOpType, mybir.ActivationFunctionType, mybir.AxisListType

    P = 128
    B, T, D = x.shape
    O = tok_w.shape[0]
    CTX = tok_w.shape[1] // D
    L = T - CTX + 1
    H, DH = 8, O // 8
    E, _, HID = w1.shape
    NT = -(-L // P)
    LAST = L - (NT - 1) * P
    LP = NT * P
    HALF = L // 2
    G = 4
    NG = B * H // G
    GB = H // G
    NPART, NPROD = 3, 6
    KR = NPROD * DH
    TT = B * NT
    FB = 4
    FT = -(-((B * L + E * (P - 1)) // P) // FB) * FB
    HC = HID // P
    EPS = 1e-5
    SCALE = float(DH) ** -0.5
    XLAST = T - (NT - 1) * P
    assert O == P and 2 * D == P and L == 2 * HALF and GB == 2 and NT == 6 and HC == 2

    Q_RUNS = [(0, 0, 3), (3, 0, 2), (5, 0, 1)]
    K_RUNS = [(0, 0, 1), (1, 0, 1), (2, 0, 1), (3, 1, 1), (4, 1, 1), (5, 2, 1)]

    parts_dram = nc.dram_tensor("parts_scratch", (2, B, H, NPART * DH, L), BF16).ap()
    xs_dram = nc.dram_tensor("sorted_tokens", (FT * P, O), F32).ap()
    ys_dram = nc.dram_tensor("sorted_results", (FT * P, O), F32).ap()

    ctx = ExitStack()
    with ctx:
        def sb(name, shape, dt=F32):
            return ctx.enter_context(nc.sbuf_tensor(name, shape, dt))

        def sem(name):
            return ctx.enter_context(nc.semaphore(name))

        ps = ctx.enter_context(nc.psum_tensor("ps", [P, 8 * 512], F32))

        def bank(i, n=512):
            return ps[:, i * 512:i * 512 + n]

        qstack = sb("qstack", [P, B * H, L], BF16)
        kstack = sb("kstack", [P, B * H, L], BF16)
        hres = sb("hres", [P, TT, O])
        v_all = sb("v_all", [P, NG, NT, G * DH])
        o_all = sb("o_all", [P, NG, LP])
        ident = sb("ident", [P, P])
        identb = sb("identb", [P, P], BF16)
        w_conv = sb("w_conv", [P, 3 * P])
        w_proj = sb("w_proj", [P, 4 * P])
        tokb_bc = sb("tokb_bc", [P, O])
        bagg_bc = sb("bagg_bc", [P, O])
        eps_t = sb("eps_t", [P, 1])
        stats = sb("stats", [P, NT, 6])
        mv = sb("mv", [P, NT, 2])
        sd = sb("sd", [P, NT])
        rstd = sb("rstd", [P, NT])
        z = sb("z", [P, NT, O])
        zt = sb("zt", [P, LP])
        x_in = sb("x_in", [P, NT, P])
        xt = sb("xt", [P, LP + 8])
        region = sb("region", [P, 4640])
        parts = region[:, 0:6 * L // 2].bitcast(BF16).rearrange("p (a c n) -> p a c n", a=2, c=NPART)
        rest = region[:, 6 * L // 2:6 * L // 2 + 2 * L].rearrange("p (a n) -> p a n", a=2)
        w_in = region[:, 0:6 * P + 64]
        probs = region[:, 0:12 * HALF].rearrange("p (s n) -> p s n", s=12)
        v_grp = sb("v_grp", [P, NT, G, 32])
        negmax = sb("negmax", [P, 2, 3, G])
        negm = sb("negm", [P, 3, G])
        negr = sb("negr", [P, 3, G])
        mparts = sb("mparts", [P, 2, 3, NPART * G], BF16)
        mrows = sb("mrows", [NPART * G, 2, 3 * P], BF16)
        two_bf16_ones = struct.unpack("<f", struct.pack("<I", 0x3F803F80))[0]
        qf = qstack[:, :, :].rearrange("p a n -> p (a n)").bitcast(F32)
        kf = kstack[:, :, :].rearrange("p a n -> p (a n)").bitcast(F32)
        z_all = qf[:, 0:TT * O].rearrange("p (t n) -> p t n", t=TT)
        y_all = qf[:, TT * O:2 * TT * O].rearrange("p (t n) -> p t n", t=TT)
        o_fin = qf[:, 2 * TT * O:3 * TT * O].rearrange("p (t n) -> p t n", t=TT)
        o_bat = kf[:, 0:2 * LP].rearrange("p (g n) -> p g n", g=2)
        w1_sb = kf[:, 1536:1536 + E * HID].rearrange("p (e n) -> p e n", e=E)
        w2_sb = kf[:, 3584:3584 + E * HID].rearrange("p (e c n) -> p e c n", e=E, c=HC)
        b1_bc = kf[:, 5632:5632 + E * HID].rearrange("p (e n) -> p e n", e=E)
        b2_bc = kf[:, 7680:7680 + E * O].rearrange("p (e n) -> p e n", e=E)
        on = kf[:, 8704:8704 + NT * O].rearrange("p (t n) -> p t n", t=NT)
        ont = kf[:, 9472:9472 + LP]
        rden = kf[:, 10240:10240 + NT * H]
        logits = kf[:, 10304:10304 + TT * E].rearrange("p (t e) -> p t e", e=E)
        bg_bc = kf[:, 10496:10496 + E]
        wg_sb = kf[:, 10504:10504 + E]
        f_x = region[:, 0:FB * O].rearrange("p (k n) -> p k n", k=FB)
        f_xt = region[:, 512:512 + FB * P].rearrange("p (k n) -> p k n", k=FB)
        f_h = region[:, 1024:1024 + FB * HID].rearrange("p (k n) -> p k n", k=FB)
        f_ht = region[:, 2048:2048 + FB * HID].rearrange("p (k c n) -> p k c n", k=FB, c=HC)
        f_y = region[:, 3072:3072 + FB * O].rearrange("p (k n) -> p k n", k=FB)
        r_max = sb("r_max", [P, TT])
        r_cand = sb("r_cand", [P, TT, E])
        r_hot = sb("r_hot", [P, TT, E])
        r_e8 = sb("r_e8", [P, E])
        r_valid = sb("r_valid", [P, TT])
        r_scan = sb("r_scan", [P, E, TT])
        r_excl = sb("r_excl", [P, E, TT])
        r_zero = sb("r_zero", [P, E * TT])
        r_cnt = sb("r_cnt", [P, E])
        r_lim = sb("r_lim", [P, TT + 1])
        r_more = sb("r_more", [P, E, TT + 1])
        r_tiles = sb("r_tiles", [P, E])
        r_upto = sb("r_upto", [P, E])
        r_off = sb("r_off", [P, E])
        r_pos = sb("r_pos", [P, TT, E])
        r_posf = sb("r_posf", [P, TT])
        r_posi = sb("r_posi", [P, TT], U32)
        r_tile_no = sb("r_tile_no", [P, FT])
        r_past = sb("r_past", [P, FT, E])
        r_expf = sb("r_expf", [P, FT])
        r_expi = sb("r_expi", [P, FT], I32)
        tri = sb("tri", [P, P])
        ones = sb("ones", [P, P])

        w_loaded, consts = sem("w_loaded"), sem("consts")
        w_t_ps, w_t_done = sem("w_t_ps"), sem("w_t_done")
        x_loaded, xt_ps, xt_done = sem("x_loaded"), sem("xt_ps"), sem("xt_done")
        conv_ps, h_done = sem("conv_ps"), sem("h_done")
        ln_chain, var_done, sd_done, z_done = sem("ln_chain"), sem("var_done"), sem("sd_done"), sem("z_done")
        zt_ps, zt_done = sem("zt_ps"), sem("zt_done")
        q_ps, k_ps, v_ps, v_done = sem("q_ps"), sem("k_ps"), sem("v_ps"), sem("v_done")
        hi_done, rest_done, mid_done, lo_done = sem("hi_done"), sem("rest_done"), sem("mid_done"), sem("lo_done")
        parts_stored, stack_loaded = sem("parts_stored"), sem("stack_loaded")
        hb_done = sem("hb_done")
        max_ps, max_done, msplit, msplit_chain = sem("max_ps"), sem("max_done"), sem("msplit"), sem("msplit_chain")
        mrow_ps, mrow_done = sem("mrow_ps"), sem("mrow_done")
        mrows_a, mrows_b = sem("mrows_a"), sem("mrows_b")
        score_ps, exp_done, pv_done, vgrp_done, o_done = (
            sem("score_ps"), sem("exp_done"), sem("pv_done"), sem("vgrp_done"), sem("o_done"))
        o_loaded, ot_ps, rden_done, on_done = sem("o_loaded"), sem("ot_ps"), sem("rden_done"), sem("on_done")
        ont_ps, ont_done, agg_ps, h2_done = sem("ont_ps"), sem("ont_done"), sem("agg_ps"), sem("h2_done")
        z2t_ps, z2t_done, log_ps, log_done = sem("z2t_ps"), sem("z2t_done"), sem("log_ps"), sem("log_done")
        ln2_chain, var2_done, sd2_done, z2_done = sem("ln2_chain"), sem("var2_done"), sem("sd2_done"), sem("z2_done")
        parts_free, fy_free = sem("parts_free"), sem("fy_free")
        zc_done, late_loaded, zeroed = sem("zc_done"), sem("late_loaded"), sem("zeroed")
        r_chain, r_hot_done, rank_ps, pos_done, expert_done = (
            sem("r_chain"), sem("r_hot_done"), sem("rank_ps"), sem("pos_done"), sem("expert_done"))
        gathered = [sem(f"gathered{b}") for b in range(B)]
        scattered, fx_loaded, fxt_ps, fxt_done = sem("scattered"), sem("fx_loaded"), sem("fxt_ps"), sem("fxt_done")
        fh_ps, fh_done, fht_ps, fht_done = sem("fh_ps"), sem("fh_done"), sem("fht_ps"), sem("fht_done")
        fy_ps, fy_done, fy_stored = sem("fy_ps"), sem("fy_done"), sem("fy_stored")
        fin_done, out_stored = sem("fin_done"), sem("out_stored")
        turns = sem("turns")
        krows_done, r_consts = sem("krows_done"), sem("r_consts")

        EXP_FREE, PV_FREE = 3, 3
        ONE_FREE = 1

        UNITS = NT * G
        X_B_AFTER, X_A_AFTER = 2, 15

        def ring_of_unit(s):
            return s + (s > X_B_AFTER) + (s > X_A_AFTER)

        X_B_RING, X_A_RING = ring_of_unit(X_B_AFTER) + 1, ring_of_unit(X_A_AFTER) + 1
        RING_ENTRY = {ring_of_unit(s): ("unit", s) for s in range(UNITS)}
        RING_ENTRY[X_B_RING] = ("x", 0)
        RING_ENTRY[X_A_RING] = ("x", 1)
        SETS = 2 * NT
        PAIRS = G * SETS
        STACK = 16 * (len(Q_RUNS) + len(K_RUNS))
        STEPS = FT // FB
        HS = NT // 2
        NG_STEPS = SETS
        NCONST = 12

        def krows(t):
            return P if t < NT - 1 else LAST

        block = ctx.enter_context(nc.Block())

        @block.sync
        def _(sp):
            sp.sem_inc(parts_free, ONE_FREE)
            sp.sem_inc(fy_free, ONE_FREE)
            sp.dma_start(w_in[:, 0:CTX * D], tok_w[:, :]).then_inc(w_loaded, 16)
            sp.dma_start(w_in[:, 320:704].rearrange("p (a n) -> p a n", a=3),
                         w_qkv.rearrange("(a p) n -> p a n", p=P)).then_inc(w_loaded, 16)
            sp.dma_start(w_in[:, 704:832], w_agg[:, :]).then_inc(w_loaded, 16)
            sp.dma_start(tokb_bc[:], tok_b.partition_broadcast(P)).then_inc(w_loaded, 16)
            sp.dma_start(bagg_bc[:], b_agg.partition_broadcast(P)).then_inc(w_loaded, 16)

            with sp.Fori(0, B) as b:
                for a in range(2):
                    for c in range(NPART):
                        if c == 0:
                            sp.wait_ge(hi_done, 2 * b + a + 1)
                            sp.sem_inc(turns, 1)
                        elif c == 1:
                            sp.wait_ge(mid_done, 2 * b + a + 1)
                            sp.sem_inc(turns, 1)
                        else:
                            sp.wait_ge(lo_done, 2 * b + a + 1)
                            sp.sem_inc(turns, 1)
                        sp.dma_start(parts_dram[a, b, :, c * DH:(c + 1) * DH, :],
                                     parts[:, a, c, :]).then_inc(parts_stored, 16)
                sp.wait_ge(parts_stored, 16 * 2 * NPART * (b + 1))
                sp.sem_inc(parts_free, 1)
                for a, dst, runs in ((0, qstack, Q_RUNS), (1, kstack, K_RUNS)):
                    for slot, c, n in runs:
                        sp.dma_start(dst[slot * DH:(slot + n) * DH, bass.ds(b * H, H), :],
                                     parts_dram[a, b, :, c * DH:(c + n) * DH, :].rearrange("h r n -> r h n")
                                     ).then_inc(stack_loaded, 16)
                sp.wait_ge(stack_loaded, STACK * (b + 1))
                sp.sem_inc(turns, 1)

            sp.wait_ge(consts, NCONST)
            sp.dma_start(xs_dram.rearrange("(t p) n -> p t n", p=P),
                         r_zero[:, 0:O].rearrange("p (a n) -> p a n", a=1).to_broadcast([P, FT, O])).then_inc(zeroed, 16)

            def max_rows(half, grp, n_done):
                cols, s = ((0, 3 * P), mrows_a) if half == 0 else ((3 * P, L), mrows_b)
                sp.wait_ge(mrow_done, n_done)
                sp.sem_inc(turns, 1)
                for c in range(NPART):
                    sp.dma_start(qstack[KR + c:KR + c + 1, bass.ds(grp * G, G), cols[0]:cols[1]],
                                 mrows[c * G:(c + 1) * G, half, 0:cols[1] - cols[0]]).then_inc(s, 16)

            max_rows(0, 0, 1)
            with sp.Fori(0, NG - 1) as g:
                max_rows(1, g, 2 * g + 2)
                max_rows(0, g + 1, 2 * g + 3)
            max_rows(1, NG - 1, 2 * NG)

            sp.wait_ge(pv_done, PV_FREE + SETS * NG)
            def load_o(b):
                sp.wait_ge(o_done, ONE_FREE + 2 * GB * (b + 1))
                sp.sem_inc(turns, 1)
                sp.dma_start(o_bat[:, :, :], o_all[:, bass.ds(b * GB, GB), :]).then_inc(o_loaded, 16)
            load_o(0)
            sp.dma_start(wg_sb, wg[:, :]).then_inc(late_loaded, 16)
            sp.dma_start(bg_bc, bg.partition_broadcast(P)).then_inc(late_loaded, 16)
            sp.dma_start(w1_sb, w1.rearrange("e d n -> d e n")).then_inc(late_loaded, 16)
            for c in range(HC):
                sp.dma_start(w2_sb[:, :, c, :], w2[:, c * P:(c + 1) * P, :].rearrange("e p n -> p e n")).then_inc(late_loaded, 16)
            sp.dma_start(b1_bc, b1.partition_broadcast(P)).then_inc(late_loaded, 16)
            sp.dma_start(b2_bc, b2.partition_broadcast(P)).then_inc(late_loaded, 16)
            with sp.Fori(1, B) as b:
                sp.wait_ge(ot_ps, b)
                sp.sem_inc(turns, 1)
                load_o(b)

            sp.wait_ge(scattered, 16 * TT)
            def load_x(i):
                sp.dma_start(f_x, xs_dram[bass.ds(i * FB * P, FB * P), :].rearrange("(k p) n -> p k n", p=P)
                             ).then_inc(fx_loaded, 16)

            def store_y(i):
                sp.wait_ge(fy_done, FB * (i + 1))
                sp.sem_inc(turns, 1)
                sp.dma_start(ys_dram[bass.ds(i * FB * P, FB * P), :].rearrange("(k p) n -> p k n", p=P),
                             f_y).then_inc(fy_stored, 16)
                sp.wait_ge(fy_stored, 16 * (i + 1))
                sp.sem_inc(fy_free, 1)

            load_x(0)
            with sp.Fori(0, STEPS - 1) as i:
                sp.wait_ge(fxt_ps, i + 1)
                sp.sem_inc(turns, 1)
                load_x(i + 1)
                store_y(i)
            store_y(STEPS - 1)

            for b in range(B):
                sp.wait_ge(fin_done, b + 1)
                sp.dma_start(out[b, 0:(NT - 1) * P, :].rearrange("(t p) n -> p t n", p=P),
                             o_fin[:, b * NT:b * NT + NT - 1, :]).then_inc(out_stored, 16)
                sp.dma_start(out[b, (NT - 1) * P:L, :], o_fin[0:LAST, b * NT + NT - 1, :]).then_inc(out_stored, 16)
            sp.wait_ge(out_stored, 16 * 2 * B)

        @block.gpsimd
        def _(pool):
            def load_x(b):
                for k, width in ((0, XLAST), (1, XLAST - 1)):
                    pool.dma_start(x_in[:, 0:NT - 1, k * D:(k + 1) * D],
                                   x[b, k:k + (NT - 1) * P, :].rearrange("(t p) d -> p t d", p=P)
                                   ).then_inc(x_loaded, 16)
                    pool.dma_start(x_in[0:width, NT - 1, k * D:(k + 1) * D],
                                   x[b, k + (NT - 1) * P:T, :]).then_inc(x_loaded, 16)

            nc.gpsimd.memset(x_in[:, NT - 1, :], 0.0).then_inc(consts, 1)
            pool.wait_ge(consts, 1)
            load_x(0)
            nc.gpsimd.memset(ident[:], 0.0).then_inc(consts, 1)
            nc.gpsimd.memset(xt[:, LP:LP + 8], 0.0).then_inc(consts, 1)
            nc.gpsimd.memset(eps_t[:], EPS).then_inc(consts, 1)
            nc.gpsimd.memset(ones[:], 1.0).then_inc(consts, 1)
            nc.gpsimd.memset(r_zero[:], 0.0).then_inc(consts, 1)
            pool.wait_ge(consts, 6)
            nc.gpsimd.affine_select(out=ident[:], in_=ident[:], compare_op=ALU.not_equal, fill=1.0, base=0,
                                    pattern=[[-1, P]], channel_multiplier=1).then_inc(consts, 1)
            pool.wait_ge(consts, 7)
            nc.gpsimd.tensor_copy(identb[:], ident[:]).then_inc(consts, 1)
            nc.gpsimd.memset(v_grp[:], 0.0).then_inc(consts, 1)
            nc.gpsimd.memset(negmax[:], 0.0).then_inc(consts, 1)
            pool.wait_ge(consts, 10)
            nc.gpsimd.memset(v_grp[:, :, :, DH:DH + 1], 1.0).then_inc(consts, 1)
            nc.gpsimd.memset(o_all[:, :, L:LP], 1.0).then_inc(consts, 1)

            def residual_bias(b):
                pool.wait_ge(w_loaded, 16 * 5)
                pool.wait_ge(z_done, b + 1)
                h = hres[:, bass.ds(b * NT, NT), :]
                nc.gpsimd.tensor_tensor(h, h, bagg_bc[:].rearrange("p (a n) -> p a n", a=1).to_broadcast([P, NT, O]),
                                        ALU.add).then_inc(hb_done, 1)

            with pool.Fori(0, B - 1) as b:
                pool.wait_ge(xt_ps, b + 1)
                load_x(b + 1)
                residual_bias(b)
            residual_bias(B - 1)

            nc.gpsimd.iota(r_e8[:], pattern=[[-1, E]], base=E, channel_multiplier=0,
                           allow_small_or_imprecise_dtypes=True).then_inc(r_consts, 1)
            nc.gpsimd.iota(r_lim[:], pattern=[[P, TT + 1]], base=0, channel_multiplier=0,
                           allow_small_or_imprecise_dtypes=True).then_inc(r_consts, 1)
            nc.gpsimd.iota(r_tile_no[:], pattern=[[1, FT]], base=0, channel_multiplier=0,
                           allow_small_or_imprecise_dtypes=True).then_inc(r_consts, 1)
            nc.gpsimd.memset(r_valid[:], 1.0).then_inc(r_consts, 1)
            pool.wait_ge(r_consts, 4)
            nc.gpsimd.affine_select(out=r_valid[:, NT - 1:TT:NT], in_=r_valid[:, NT - 1:TT:NT], compare_op=ALU.is_ge,
                                    fill=0.0, base=LAST - 1, pattern=[[0, B]],
                                    channel_multiplier=-1).then_inc(r_consts, 1)
            nc.gpsimd.affine_select(out=tri[:], in_=ones[:], compare_op=ALU.is_gt, fill=0.0, base=0,
                                    pattern=[[1, P]], channel_multiplier=-1).then_inc(r_consts, 1)

            def split_maxima(half, grp, idx):
                pool.wait_ge(max_done, UNITS * grp + HS * G * (half + 1))
                pool.sem_inc(turns, 1)
                src, dst = negmax[:, half, :, :], mparts[:, half, :, :]
                nc.gpsimd.tensor_copy(dst[:, :, 0:G], src).then_inc(msplit_chain, 1)
                pool.wait_ge(msplit_chain, 3 * idx + 1)
                nc.gpsimd.tensor_tensor(negr[:], src, dst[:, :, 0:G], ALU.subtract).then_inc(msplit_chain, 1)
                pool.wait_ge(msplit_chain, 3 * idx + 2)
                pool.sem_inc(turns, 1)
                nc.gpsimd.tensor_copy(dst[:, :, G:2 * G], negr[:]).then_inc(msplit_chain, 1)
                pool.wait_ge(msplit_chain, 3 * idx + 3)
                nc.gpsimd.tensor_tensor(dst[:, :, 2 * G:3 * G], negr[:], dst[:, :, G:2 * G],
                                        ALU.subtract).then_inc(msplit, 1)

            def copy_values(grp, t):
                nc.gpsimd.tensor_copy(v_grp[:, t, :, 0:DH],
                                      v_all[:, grp, t, :].rearrange("p (h d) -> p h d", h=G)).then_inc(vgrp_done, 1)

            pool.wait_ge(v_done, 1)
            for t in range(NT):
                copy_values(0, t)
            split_maxima(0, 0, 0)
            split_maxima(1, 0, 1)
            with pool.Fori(0, NG - 1) as g:
                split_maxima(0, g + 1, 2 * g + 2)
                for t in range(NT):
                    if t == NT - 2:
                        split_maxima(1, g + 1, 2 * g + 3)
                    pool.wait_ge(pv_done, SETS * g + PV_FREE + NT + t + 1)
                    pool.sem_inc(turns, 1)
                    copy_values(g + 1, t)

            pool.sem_inc(zc_done, ONE_FREE)
            with pool.Fori(0, B) as b:
                pool.wait_ge(z2_done, b + 1)
                pool.sem_inc(turns, 1)
                nc.gpsimd.tensor_copy(z_all[:, bass.ds(b * NT, NT), :], z[:]).then_inc(zc_done, 1)

            pool.wait_ge(zc_done, ONE_FREE + B)
            pool.wait_ge(zeroed, 16)
            pool.wait_ge(pos_done, 1)
            for t in range(TT):
                n = krows(t % NT)
                pool.indirect_dma_start(out=xs_dram[:, :],
                                        out_offset=bass.IndirectOffsetOnAxis(ap=r_posi[0:n, t:t + 1], axis=0),
                                        in_=z_all[0:n, t, :], in_offset=None).then_inc(scattered, 16)
            pool.wait_ge(fy_stored, 16 * STEPS)
            for t in range(TT):
                n = krows(t % NT)
                pool.indirect_dma_start(out=y_all[0:n, t, :], out_offset=None, in_=ys_dram[:, :],
                                        in_offset=bass.IndirectOffsetOnAxis(ap=r_posi[0:n, t:t + 1], axis=0)
                                        ).then_inc(gathered[t // NT], 16)

        @block.scalar
        def _(act):
            act.wait_ge(w_t_ps, 1)
            nc.scalar.copy(w_conv[:, 0:2 * P], bank(0, 2 * P)).then_inc(w_t_done, 1)
            nc.scalar.copy(w_conv[0:D, 2 * P:3 * P], ps[0:D, 2 * P:3 * P]).then_inc(w_t_done, 1)
            nc.scalar.copy(w_proj[:], bank(1)).then_inc(w_t_done, 1)

            def copy_xt(b):
                act.wait_ge(xt_ps, b + 1)
                nc.scalar.copy(xt[:, 0:LP], ps[:, 0:LP]).then_inc(xt_done, 1)

            def sqrt_var(b, var, done):
                act.wait_ge(var, b + 1)
                nc.scalar.activation(sd[:], mv[:, :, 1], ACT.Sqrt, bias=eps_t[:]).then_inc(done, 1)

            def qkv_copies(b):
                act.wait_ge(zt_ps, b + 1)
                nc.scalar.copy(zt[:], ps[:, 4 * 512:4 * 512 + LP]).then_inc(zt_done, 1)
                act.wait_ge(parts_free, b + 1)
                for a, (ready, first) in enumerate(((q_ps, 6), (k_ps, 4))):
                    act.wait_ge(ready, b + 1)
                    nc.scalar.copy(parts[:, a, 0, :].rearrange("p (c n) -> p c n", c=2),
                                   ps[:, first * 512:(first + 2) * 512].rearrange("p (c n) -> p c n", c=2)[:, :, 0:HALF]
                                   ).then_inc(hi_done, 1)
                for a in range(2):
                    act.wait_ge(rest_done, 2 * b + a + 1)
                    nc.scalar.copy(parts[:, a, 1, :], rest[:, a, :]).then_inc(mid_done, 1)
                act.wait_ge(v_ps, b + 1)
                nc.scalar.copy(v_all[:, bass.ds(b * GB, GB), :, :].rearrange("p g t n -> p t g n"),
                               ps[:, 6 * 512:6 * 512 + LP].rearrange("p (t g n) -> p t g n", t=NT, g=GB)
                               ).then_inc(v_done, 1)

            act.wait_ge(consts, NCONST)
            copy_xt(0)
            with act.Fori(0, B - 1) as b:
                copy_xt(b + 1)
                sqrt_var(b, var_done, sd_done)
                qkv_copies(b)
            sqrt_var(B - 1, var_done, sd_done)
            qkv_copies(B - 1)

            act.sem_inc(exp_done, EXP_FREE)
            act.sem_inc(o_done, ONE_FREE)

            def copy_max_rows(half, idx):
                act.wait_ge(mrow_ps, idx + 1)
                r = X_A_RING if half == 0 else X_B_RING
                nc.scalar.copy(mrows[:, half, :],
                               bank(2 * (r % 2)).bitcast(BF16)[0:NPART * G, 0:HS * P]).then_inc(mrow_done, 1)

            def exponentials(g, last):
                for s in range(UNITS):
                    for a in range(2):
                        k = 2 * s + a
                        rows = krows((s % NG_STEPS) // 2)
                        if k % G == 0:
                            act.wait_ge(pv_done, SETS * g + k // G + 1)
                        act.wait_ge(score_ps, PAIRS * g + k + 1)
                        nc.scalar.activation(probs[0:rows, k % 12, :], ps[0:rows, (4 + k % 3) * 512:(4 + k % 3) * 512 + HALF],
                                             ACT.Exp, scale=SCALE).then_inc(exp_done, 1)
                    if s == X_B_AFTER + 2:
                        copy_max_rows(1, 2 * g + 1)
                    if s == X_A_AFTER + 2 and not last:
                        copy_max_rows(0, 2 * g + 2)
                    if s == NG_STEPS + 1:
                        copy_outputs(g, 0)
                copy_outputs(g, 1)

            def copy_outputs(g, half):
                act.wait_ge(pv_done, SETS * g + PV_FREE + NT * (half + 1))
                nc.scalar.copy(o_all[:, g, half * HALF:(half + 1) * HALF], bank(7, HALF)).then_inc(o_done, 1)

            copy_max_rows(0, 0)
            act.wait_ge(parts_free, B + 1)
            with act.Fori(0, NG - 1) as g:
                exponentials(g, False)
            exponentials(NG - 1, True)

            def copy_ont(b):
                act.wait_ge(ont_ps, b + 1)
                nc.scalar.copy(ont, ps[:, 3 * 512:3 * 512 + LP]).then_inc(ont_done, 1)

            def copy_z2t(b):
                act.wait_ge(z2t_ps, b + 1)
                nc.scalar.copy(zt[:], ps[:, 3 * 512:3 * 512 + LP]).then_inc(z2t_done, 1)

            copy_ont(0)
            with act.Fori(0, B - 1) as b:
                copy_ont(b + 1)
                sqrt_var(b, var2_done, sd2_done)
                copy_z2t(b)
            sqrt_var(B - 1, var2_done, sd2_done)
            copy_z2t(B - 1)

            with act.Fori(0, STEPS) as i:
                act.wait_ge(fxt_ps, i + 1)
                nc.scalar.copy(f_xt, bank(0).rearrange("p (k n) -> p k n", k=FB)).then_inc(fxt_done, 1)
                for p in range(FB // 2):
                    act.wait_ge(fht_ps, 2 * i + p + 1)
                    nc.scalar.activation(f_ht[:, 2 * p:2 * p + 2, :, :],
                                         bank(3 + p).rearrange("p (k c n) -> p k c n", k=2, c=HC), ACT.Relu
                                         ).then_inc(fht_done, 1)

        @block.vector
        def _(dve):
            def ln_stats(src, chain, n, var):
                for t in range(NT):
                    last = nc.vector.bn_stats(stats[:, t, :], src(t))
                last.then_inc(chain, 1)
                dve.wait_ge(chain, n)
                dve.sem_inc(turns, 1)
                for t in range(NT):
                    last = nc.vector.bn_aggr(mv[:, t, :], stats[:, t, :])
                last.then_inc(var, 1)

            def ln_apply(src, chain, n, var, b, sdev, done):
                dve.wait_ge(sdev, b + 1)
                dve.wait_ge(var, b + 1)
                nc.vector.reciprocal(rstd[:], sd[:]).then_inc(chain, 1)
                dve.wait_ge(chain, n)
                for t in range(NT):
                    last = nc.vector.tensor_scalar(z[:, t, :], src(t), mv[:, t, 0:1], rstd[:, t:t + 1],
                                                   ALU.subtract, ALU.mult)
                last.then_inc(done, 1)

            def h_tile(b):
                return lambda t: hres[:, b * NT + t, :]

            nc.vector.memset(kf[KR:KR + NPART, :], two_bf16_ones).then_inc(krows_done, 1)

            def add_conv_bias(b):
                dve.wait_ge(conv_ps, b + 1)
                nc.vector.tensor_tensor(hres[:, bass.ds(b * NT, NT), :],
                                        ps[:, 2 * 512:2 * 512 + LP].rearrange("p (t n) -> p t n", t=NT),
                                        tokb_bc[:].rearrange("p (a n) -> p a n", a=1).to_broadcast([P, NT, O]),
                                        ALU.add).then_inc(h_done, 1)

            def layer_norm_1(b):
                dve.wait_ge(h_done, b + 1)
                ln_stats(h_tile(b), ln_chain, 2 * b + 1, var_done)
                ln_apply(h_tile(b), ln_chain, 2 * b + 2, var_done, b, sd_done, z_done)

            def thirds(b):
                for a, first in enumerate((6, 4)):
                    dve.wait_ge(hi_done, 2 * b + a + 1)
                    nc.vector.tensor_tensor(rest[:, a, :].rearrange("p (c n) -> p c n", c=2),
                                            ps[:, first * 512:(first + 2) * 512].rearrange("p (c n) -> p c n", c=2)[:, :, 0:HALF],
                                            parts[:, a, 0, :].rearrange("p (c n) -> p c n", c=2),
                                            ALU.subtract).then_inc(rest_done, 1)
                for a in range(2):
                    dve.wait_ge(mid_done, 2 * b + a + 1)
                    nc.vector.tensor_tensor(parts[:, a, 2, :], rest[:, a, :], parts[:, a, 1, :],
                                            ALU.subtract).then_inc(lo_done, 1)

            dve.wait_ge(w_loaded, 16 * 5)
            add_conv_bias(0)
            with dve.Fori(0, B - 1) as b:
                layer_norm_1(b)
                add_conv_bias(b + 1)
                thirds(b)
            layer_norm_1(B - 1)
            thirds(B - 1)

            def maxima(grp):
                for s in range(UNITS):
                    t, h = s // G, s % G
                    first = 2 * (ring_of_unit(s) % 2)
                    rows = krows(t)
                    dve.wait_ge(max_ps, UNITS * grp + s + 1)
                    nc.vector.tensor_reduce(negmax[0:rows, t // HS, t % HS, h:h + 1],
                                            ps[0:rows, first * 512:(first + 2) * 512].rearrange("p (c n) -> p c n", c=2)[:, :, 0:HALF],
                                            axis=AX.XY, op=ALU.max, negate=True).then_inc(max_done, 1)

            dve.wait_ge(consts, NCONST)
            maxima(0)
            with dve.Fori(0, NG - 1) as g:
                maxima(g + 1)

            def normalise(b):
                dve.wait_ge(ot_ps, b + 1)
                heads = ps[:, 0:NT * H * 32].rearrange("p (a n) -> p a n", n=32)
                nc.vector.reciprocal(rden, heads[:, :, DH]).then_inc(rden_done, 1)
                dve.wait_ge(rden_done, b + 1)
                nc.vector.tensor_tensor(on.rearrange("p t (h d) -> p (t h) d", d=DH), heads[:, :, 0:DH],
                                        rden.rearrange("p (a n) -> p a n", n=1).to_broadcast([P, NT * H, DH]),
                                        ALU.mult).then_inc(on_done, 1)

            def add_residual(b):
                dve.wait_ge(agg_ps, b + 1)
                h = hres[:, bass.ds(b * NT, NT), :]
                nc.vector.tensor_tensor(h, ps[:, 5 * 512:5 * 512 + LP].rearrange("p (t n) -> p t n", t=NT), h,
                                        ALU.add).then_inc(h2_done, 1)

            def router_logits(b):
                dve.wait_ge(log_ps, b + 1)
                nc.vector.tensor_tensor(logits[:, bass.ds(b * NT, NT), :],
                                        bank(7, NT * E).rearrange("p (t e) -> p t e", e=E),
                                        bg_bc.rearrange("p (a e) -> p a e", a=1).to_broadcast([P, NT, E]),
                                        ALU.add).then_inc(log_done, 1)

            def layer_norm_2a(b):
                dve.wait_ge(h2_done, b + 1)
                ln_stats(h_tile(b), ln2_chain, 2 * b + 1, var2_done)

            def layer_norm_2b(b):
                dve.wait_ge(zc_done, ONE_FREE + b)
                ln_apply(h_tile(b), ln2_chain, 2 * b + 2, var2_done, b, sd2_done, z2_done)

            dve.wait_ge(hb_done, B)
            dve.wait_ge(late_loaded, 16 * 7)
            normalise(0)
            add_residual(0)
            with dve.Fori(0, B - 1) as b:
                normalise(b + 1)
                layer_norm_2a(b)
                add_residual(b + 1)
                layer_norm_2b(b)
                router_logits(b)
            layer_norm_2a(B - 1)
            layer_norm_2b(B - 1)
            router_logits(B - 1)

            chain = [0]

            def link(ins):
                chain[0] += 1
                ins.then_inc(r_chain, 1)
                dve.wait_ge(r_chain, chain[0])

            def over_e(ap, n):
                return ap.rearrange("p (n a) -> p n a", a=1).to_broadcast([P, n, E])

            dve.wait_ge(r_consts, 6)
            dve.wait_ge(log_done, B)
            link(nc.vector.tensor_reduce(r_max[:], logits, axis=AX.X, op=ALU.max))
            link(nc.vector.tensor_tensor(r_cand[:], logits, over_e(r_max[:], TT), ALU.is_equal))
            link(nc.vector.tensor_tensor(r_cand[:], r_cand[:], r_e8[:].rearrange("p (a e) -> p a e", a=1)
                                         .to_broadcast([P, TT, E]), ALU.mult))
            link(nc.vector.tensor_reduce(r_max[:], r_cand[:], axis=AX.X, op=ALU.max))
            link(nc.vector.tensor_tensor(r_hot[:], r_cand[:], over_e(r_max[:], TT), ALU.is_equal))
            nc.vector.tensor_tensor(r_hot[:], r_hot[:], over_e(r_valid[:], TT), ALU.mult).then_inc(r_hot_done, 1)
            dve.wait_ge(rank_ps, 1)
            totals = bank(1, TT * E).rearrange("p (t e) -> p e t", e=E)
            link(nc.vector.tensor_copy(r_excl[:], totals))
            link(nc.vector.tensor_reduce(r_cnt[:], r_excl[:], axis=AX.X, op=ALU.add))
            link(nc.vector.tensor_tensor(r_more[:], r_cnt[:].rearrange("p (e a) -> p e a", a=1).to_broadcast([P, E, TT + 1]),
                                         r_lim[:].rearrange("p (a n) -> p a n", a=1).to_broadcast([P, E, TT + 1]), ALU.is_gt))
            link(nc.vector.tensor_reduce(r_tiles[:], r_more[:], axis=AX.X, op=ALU.add))
            link(nc.vector.tensor_tensor_scan(out=r_upto[:], data0=r_zero[:, 0:E], data1=r_tiles[:], initial=0.0,
                                              op0=ALU.add, op1=ALU.add))
            flat = r_excl[:].rearrange("p e t -> p (e t)")
            link(nc.vector.tensor_tensor_scan(out=r_scan[:].rearrange("p e t -> p (e t)"), data0=r_zero[:], data1=flat,
                                              initial=0.0, op0=ALU.add, op1=ALU.add))
            link(nc.vector.tensor_tensor(r_excl[:], r_scan[:], r_excl[:], ALU.subtract))
            link(nc.vector.tensor_tensor(r_off[:], r_upto[:], r_tiles[:], ALU.subtract))
            link(nc.vector.scalar_tensor_tensor(out=r_off[:], in0=r_off[:], scalar=float(P), in1=r_excl[:, :, 0],
                                                op0=ALU.mult, op1=ALU.subtract))
            link(nc.vector.tensor_tensor(r_pos[:], bank(0, TT * E).rearrange("p (t e) -> p t e", e=E),
                                         r_excl[:].rearrange("p e t -> p t e"), ALU.add))
            link(nc.vector.tensor_tensor(r_pos[:], r_pos[:], r_off[:].rearrange("p (a e) -> p a e", a=1)
                                         .to_broadcast([P, TT, E]), ALU.add))
            link(nc.vector.tensor_tensor(r_pos[:], r_pos[:], r_hot[:], ALU.mult))
            link(nc.vector.tensor_reduce(r_posf[:], r_pos[:], axis=AX.X, op=ALU.add))
            nc.vector.tensor_copy(r_posi[:], r_posf[:]).then_inc(pos_done, 1)
            link(nc.vector.tensor_tensor(r_past[:], over_e(r_tile_no[:], FT),
                                         r_upto[:].rearrange("p (a e) -> p a e", a=1).to_broadcast([P, FT, E]), ALU.is_ge))
            link(nc.vector.tensor_reduce(r_expf[:], r_past[:], axis=AX.X, op=ALU.add))
            link(nc.vector.tensor_scalar(r_expf[:], r_expf[:], float(E - 1), None, ALU.min))
            nc.vector.tensor_copy(r_expi[:], r_expf[:]).then_inc(expert_done, 1)
            dve.wait_ge(expert_done, 1)

            with dve.Fori(0, STEPS) as i:
                e = [dve.value_load(r_expi[0:1, bass.ds(i * FB + k, 1)], min_val=0, max_val=E - 1) for k in range(FB)]
                for p in range(FB // 2):
                    dve.wait_ge(fh_ps, 2 * i + p + 1)
                    for k in (2 * p, 2 * p + 1):
                        nc.vector.tensor_tensor(f_h[:, k, :], bank(1 + p)[:, (k % 2) * HID:(k % 2 + 1) * HID],
                                                b1_bc[:, e[k], :], ALU.add).then_inc(fh_done, 1)
                dve.wait_ge(fy_free, i + 1)
                for p in range(FB // 2):
                    dve.wait_ge(fy_ps, 2 * i + p + 1)
                    for k in (2 * p, 2 * p + 1):
                        nc.vector.tensor_tensor(f_y[:, k, :], bank(5 + p)[:, (k % 2) * O:(k % 2 + 1) * O],
                                                b2_bc[:, e[k], :], ALU.add).then_inc(fy_done, 1)

            for b in range(B):
                dve.wait_ge(gathered[b], 16 * NT)
                first, end = b * NT, b * NT + NT - 1
                nc.vector.tensor_tensor(o_fin[:, first:end, :], y_all[:, first:end, :], hres[:, first:end, :], ALU.add)
                nc.vector.tensor_tensor(o_fin[0:LAST, end, :], y_all[0:LAST, end, :], hres[0:LAST, end, :],
                                        ALU.add).then_inc(fin_done, 1)

        @block.tensor
        def _(pe):
            pe.wait_ge(consts, NCONST)
            pe.wait_ge(w_loaded, 16 * 5)
            for c in range(3):
                w = min(P, CTX * D - c * P)
                nc.tensor.transpose(ps[0:w, c * P:(c + 1) * P], w_in[:, c * P:c * P + w], ident[:])
            for c in range(4):
                last = nc.tensor.transpose(bank(1)[:, c * P:(c + 1) * P], w_in[:, 320 + c * P:320 + (c + 1) * P], ident[:])
            last.then_inc(w_t_ps, 1)
            pe.wait_ge(w_t_done, 3)

            def transpose_x(b):
                pe.wait_ge(x_loaded, 16 * 4 * (b + 1))
                for t in range(NT):
                    last = nc.tensor.transpose(ps[:, t * P:(t + 1) * P], x_in[:, t, :], ident[:])
                last.then_inc(xt_ps, 1)

            def convolve(b, first=False):
                pe.wait_ge(xt_done, b + 1)
                if not first:
                    pe.wait_ge(h_done, b)
                for t in range(NT):
                    dst = ps[:, 2 * 512 + t * P:2 * 512 + (t + 1) * P]
                    nc.tensor.matmul(dst, xt[:, t * P:(t + 1) * P], w_conv[:, 0:P], start=True, stop=False)
                    nc.tensor.matmul(dst, xt[:, t * P + 2:(t + 1) * P + 2], w_conv[:, P:2 * P], start=False, stop=False)
                    last = nc.tensor.matmul(dst, xt[0:D, t * P + 4:(t + 1) * P + 4], w_conv[0:D, 2 * P:3 * P],
                                            start=False, stop=True)
                last.then_inc(conv_ps, 1)

            def project(b):
                pe.wait_ge(z_done, b + 1)
                for t in range(NT):
                    last = nc.tensor.transpose(ps[:, 4 * 512 + t * P:4 * 512 + (t + 1) * P], z[:, t, :], ident[:])
                last.then_inc(zt_ps, 1)
                pe.wait_ge(zt_done, b + 1)
                for a, (done, first) in enumerate(((q_ps, 6), (k_ps, 4))):
                    for c in range(2):
                        last = nc.tensor.matmul(bank(first + c, HALF), w_proj[:, a * P:(a + 1) * P],
                                                zt[:, c * HALF:(c + 1) * HALF], start=True, stop=True)
                    last.then_inc(done, 1)
                pe.wait_ge(rest_done, 2 * b + 1)
                for t in range(NT):
                    last = nc.tensor.matmul(ps[:, 6 * 512 + t * P:6 * 512 + (t + 1) * P], zt[:, t * P:(t + 1) * P],
                                            w_proj[:, 2 * P:3 * P], start=True, stop=True)
                last.then_inc(v_ps, 1)

            transpose_x(0)
            convolve(0, first=True)
            with pe.Fori(0, B - 1) as b:
                transpose_x(b + 1)
                convolve(b + 1)
                project(b)
            project(B - 1)

            def score_unit(grp, s, slot_g):
                t, h = s // G, s % G
                r = ring_of_unit(s)
                before = r - 2
                while before >= 0 and RING_ENTRY[before][0] == "x" and slot_g is None and before == X_B_RING:
                    before -= 2
                if before >= 0:
                    kind, n = RING_ENTRY[before]
                    if kind == "unit":
                        pe.wait_ge(max_done, UNITS * grp + n + 1)
                    else:
                        pe.wait_ge(mrow_done, 2 * grp + n)
                elif slot_g is not None:
                    pe.wait_ge(max_done, UNITS * grp - 1 + before + 2)
                rows = krows(t)
                for c in range(2):
                    last = nc.tensor.matmul(ps[0:rows, (2 * (r % 2) + c) * 512:(2 * (r % 2) + c) * 512 + HALF],
                                            qstack[0:KR, grp * G + h, t * P:t * P + rows],
                                            kstack[0:KR, grp * G + h, c * HALF:(c + 1) * HALF], start=True, stop=True)
                last.then_inc(max_ps, 1)

            def transpose_maxima(half, idx, wait_for):
                r = X_A_RING if half == 0 else X_B_RING
                pe.wait_ge(msplit, idx + 1)
                if wait_for is not None:
                    pe.wait_ge(max_done, wait_for)
                for t in range(HS):
                    last = nc.tensor.transpose(bank(2 * (r % 2)).bitcast(BF16)[0:NPART * G, t * P:(t + 1) * P],
                                               mparts[:, half, t, :], identb[:])
                last.then_inc(mrow_ps, 1)

            def transposed_scores(g, s):
                half, t = s // NG_STEPS, (s % NG_STEPS) // 2
                rows = krows(t)
                if s == 0:
                    pe.wait_ge(mrows_a, 16 * NPART * (g + 1))
                if s == NG_STEPS:
                    pe.wait_ge(mrows_b, 16 * NPART * (g + 1))
                for a in range(2):
                    k = 2 * s + a
                    h = k % G
                    pe.wait_ge(exp_done, PAIRS * g + k + 1)
                    nc.tensor.matmul(ps[0:rows, (4 + k % 3) * 512:(4 + k % 3) * 512 + HALF],
                                     kstack[0:KR + NPART, g * G + h, t * P:t * P + rows],
                                     qstack[0:KR + NPART, g * G + h, half * HALF:(half + 1) * HALF],
                                     start=True, stop=True).then_inc(score_ps, 1)

            def value_products(g, n):
                half, t = n // NT, n % NT
                rows = krows(t)
                pe.wait_ge(exp_done, PAIRS * g + G * (n + 1) + EXP_FREE)
                if half == 0:
                    pe.wait_ge(vgrp_done, NT * g + t + 1)
                if t == 0:
                    pe.wait_ge(o_done, 2 * g + half + 1)
                for h in range(G):
                    last = nc.tensor.matmul(ps[32 * h:32 * (h + 1), 7 * 512:7 * 512 + HALF], v_grp[0:rows, t, h, :],
                                            probs[0:rows, (G * n + h) % 12, :], start=(t == 0), stop=(t == NT - 1))
                last.then_inc(pv_done, 1)

            def group(g, last):
                for s in range(UNITS):
                    transposed_scores(g, s)
                    if s % 2 == 1 and s > 1:
                        value_products(g, (s - 1) // 2 - 1)
                    if not last:
                        score_unit(g + 1, s, g)
                    if s == X_B_AFTER:
                        transpose_maxima(1, 2 * g + 1, UNITS * (g + 1) + X_B_RING - 2 + 1 if not last else UNITS * (g + 1))
                    if s == X_A_AFTER and not last:
                        transpose_maxima(0, 2 * g + 2, UNITS * (g + 1) + X_A_AFTER)
                value_products(g, SETS - 1)

            pe.sem_inc(pv_done, PV_FREE)
            pe.wait_ge(stack_loaded, STACK)
            for s in range(UNITS):
                score_unit(0, s, None)
                if s == X_A_AFTER:
                    transpose_maxima(0, 0, X_A_AFTER)
            pe.wait_ge(stack_loaded, STACK * B)
            pe.wait_ge(krows_done, 1)
            pe.wait_ge(v_done, B)
            pe.wait_ge(lo_done, 2 * B)
            with pe.Fori(0, NG - 1) as g:
                group(g, False)
            group(NG - 1, True)
            pe.wait_ge(o_done, ONE_FREE + 2 * NG)

            def transpose_o(b):
                pe.wait_ge(o_loaded, 16 * (b + 1))
                for t in range(NT):
                    for g in range(GB):
                        last = nc.tensor.transpose(ps[:, t * 256 + g * P:t * 256 + (g + 1) * P],
                                                   o_bat[:, g, t * P:(t + 1) * P], ident[:])
                last.then_inc(ot_ps, 1)

            def output_projection(b):
                pe.wait_ge(on_done, b + 1)
                for t in range(NT):
                    last = nc.tensor.transpose(ps[:, 3 * 512 + t * P:3 * 512 + (t + 1) * P], on[:, t, :], ident[:])
                last.then_inc(ont_ps, 1)
                pe.wait_ge(ont_done, b + 1)
                for t in range(NT):
                    last = nc.tensor.matmul(ps[:, 5 * 512 + t * P:5 * 512 + (t + 1) * P], ont[:, t * P:(t + 1) * P],
                                            w_proj[:, 3 * P:4 * P], start=True, stop=True)
                last.then_inc(agg_ps, 1)

            def router(b):
                pe.wait_ge(z2_done, b + 1)
                for t in range(NT):
                    last = nc.tensor.transpose(ps[:, 3 * 512 + t * P:3 * 512 + (t + 1) * P], z[:, t, :], ident[:])
                last.then_inc(z2t_ps, 1)
                pe.wait_ge(z2t_done, b + 1)
                for t in range(NT):
                    last = nc.tensor.matmul(bank(7)[:, t * E:(t + 1) * E], zt[:, t * P:(t + 1) * P], wg_sb,
                                            start=True, stop=True)
                last.then_inc(log_ps, 1)

            transpose_o(0)
            output_projection(0)
            pe.wait_ge(late_loaded, 16 * 7)
            with pe.Fori(0, B - 1) as b:
                transpose_o(b + 1)
                output_projection(b + 1)
                router(b)
            router(B - 1)

            pe.wait_ge(r_hot_done, 1)
            hot = r_hot[:].rearrange("p t e -> p (t e)")
            nc.tensor.matmul(bank(0, TT * E), tri[:], hot, start=True, stop=True)
            nc.tensor.matmul(bank(1, TT * E), ones[:], hot, start=True, stop=True).then_inc(rank_ps, 1)
            pe.wait_ge(expert_done, 1)

            with pe.Fori(0, STEPS) as i:
                e = [pe.value_load(r_expi[0:1, bass.ds(i * FB + k, 1)], min_val=0, max_val=E - 1) for k in range(FB)]
                pe.wait_ge(fx_loaded, 16 * (i + 1))
                for k in range(FB):
                    last = nc.tensor.transpose(bank(0)[:, k * P:(k + 1) * P], f_x[:, k, :], ident[:])
                last.then_inc(fxt_ps, 1)
                pe.wait_ge(fxt_done, i + 1)
                for p in range(FB // 2):
                    for k in (2 * p, 2 * p + 1):
                        last = nc.tensor.matmul(bank(1 + p)[:, (k % 2) * HID:(k % 2 + 1) * HID], f_xt[:, k, :],
                                                w1_sb[:, e[k], :], start=True, stop=True)
                    last.then_inc(fh_ps, 1)
                for p in range(FB // 2):
                    pe.wait_ge(fh_done, FB * i + 2 * p + 2)
                    for k in (2 * p, 2 * p + 1):
                        for c in range(HC):
                            last = nc.tensor.transpose(bank(3 + p)[:, ((k % 2) * HC + c) * P:((k % 2) * HC + c + 1) * P],
                                                       f_h[:, k, c * P:(c + 1) * P], ident[:])
                    last.then_inc(fht_ps, 1)
                for p in range(FB // 2):
                    pe.wait_ge(fht_done, 2 * i + p + 1)
                    for k in (2 * p, 2 * p + 1):
                        for c in range(HC):
                            last = nc.tensor.matmul(bank(5 + p)[:, (k % 2) * O:(k % 2 + 1) * O], f_ht[:, k, c, :],
                                                    w2_sb[:, e[k], c, :], start=(c == 0), stop=(c == HC - 1))
                    last.then_inc(fy_ps, 1)


_INS = ["x", "L0_tok_W", "L0_tok_b", "L0_attn_w_qkv", "L0_attn_w_agg", "L0_attn_b_agg",
        "L0_ffn_W1", "L0_ffn_b1", "L0_ffn_W2", "L0_ffn_b2", "L0_ffn_Wg", "L0_ffn_bg"]


def kernel(**inputs):
    import numpy as _np
    import concourse.bacc as _bacc
    from concourse import mybir as _mybir
    from concourse.bass_utils import run_bass_kernel_spmd as _run

    nc = _bacc.Bacc("TRN2", target_bir_lowering=False, num_devices=1)
    arrays, args = {}, []
    for name in _INS:
        a = _np.ascontiguousarray(inputs[name])
        arrays[f"in_{name}"] = a
        args.append(nc.dram_tensor(f"in_{name}", a.shape, _mybir.dt.from_np(a.dtype), kind="ExternalInput").ap())
    batches, steps, width = inputs["x"].shape
    model, taps = inputs["L0_tok_W"].shape
    shape = (batches, steps - taps // width + 1, model)
    out = nc.dram_tensor("out", shape, _mybir.dt.float32, kind="ExternalOutput").ap()
    _program(nc, *args, out)
    return _run(nc, [arrays], core_ids=[0]).results[0]["out"]
```

```python
import struct
from contextlib import ExitStack

import concourse.bass as bass
from concourse import mybir


def _program(nc, x, tok_w, tok_b, w_qkv, w_agg, b_agg, w1, b1, w2, b2, wg, bg, out):
    F32, BF16 = mybir.dt.float32, mybir.dt.bfloat16
    I32, U32 = mybir.dt.int32, mybir.dt.uint32
    ALU, ACT, AX = mybir.AluOpType, mybir.ActivationFunctionType, mybir.AxisListType

    P = 128
    B, T, D = x.shape
    O = tok_w.shape[0]
    CTX = tok_w.shape[1] // D
    L = T - CTX + 1
    H, DH = 8, O // 8
    E, _, HID = w1.shape
    NT = -(-L // P)
    LAST = L - (NT - 1) * P
    LP = NT * P
    HALF = L // 2
    G = 4
    NG = B * H // G
    GB = H // G
    NPART, NPROD = 3, 6
    KR = NPROD * DH
    TT = B * NT
    FT = ((B * L + E * (P - 1)) // P + 1) // 2 * 2
    NPAIR = FT // 2
    ROW = 2 * O + 1
    HC = HID // P
    EPS = 1e-5
    SCALE = float(DH) ** -0.5
    XLAST = T - (NT - 1) * P
    assert O == P and 2 * D == P and L == 2 * HALF and GB == 2 and NT == 6 and HC == 2

    Q_RUNS = [(0, 0, 3), (3, 0, 2), (5, 0, 1)]
    K_RUNS = [(0, 0, 1), (1, 0, 1), (2, 0, 1), (3, 1, 1), (4, 1, 1), (5, 2, 1)]

    parts_dram = nc.dram_tensor("parts_scratch", (2, B, H, NPART * DH, L), BF16).ap()
    xs_dram = nc.dram_tensor("sorted_tokens", (FT * P, ROW), F32).ap()

    ctx = ExitStack()
    with ctx:
        def sb(name, shape, dt=F32):
            return ctx.enter_context(nc.sbuf_tensor(name, shape, dt))

        def sem(name):
            return ctx.enter_context(nc.semaphore(name))

        ps = ctx.enter_context(nc.psum_tensor("ps", [P, 8 * 512], F32))

        def bank(i, n=512):
            return ps[:, i * 512:i * 512 + n]

        qstack = sb("qstack", [P, B * H, L], BF16)
        kstack = sb("kstack", [P, B * H, L], BF16)
        hres = sb("hres", [P, TT, O])
        v_all = sb("v_all", [P, NG, NT, G * DH])
        o_all = sb("o_all", [P, NG, LP])
        ident = sb("ident", [P, P])
        identb = sb("identb", [P, P], BF16)
        w_conv = sb("w_conv", [P, 3 * P])
        w_proj = sb("w_proj", [P, 4 * P])
        tokb_bc = sb("tokb_bc", [P, O])
        bagg_bc = sb("bagg_bc", [P, O])
        stats = sb("stats", [P, NT, 6])
        mv = sb("mv", [P, NT, 2])
        veps = sb("veps", [P, NT])
        nmean = sb("nmean", [P, NT])
        rstd = sb("rstd", [P, NT])
        nmr = sb("nmr", [P, NT])
        minus_half = sb("minus_half", [P, NT])
        z = sb("z", [P, NT, O])
        zt = sb("zt", [P, LP])
        x_in = sb("x_in", [P, NT, P])
        xt = sb("xt", [P, LP + 8])
        fill = x_in[:, :, :].rearrange("p t n -> p (t n)")[:, 0:ROW]
        region = sb("region", [P, 4640])
        parts = region[:, 0:6 * L // 2].bitcast(BF16).rearrange("p (a c n) -> p a c n", a=2, c=NPART)
        rest = region[:, 6 * L // 2:6 * L // 2 + 2 * L].rearrange("p (a n) -> p a n", a=2)
        w_in = region[:, 0:6 * P + 64]
        probs = region[:, 0:12 * HALF].rearrange("p (s n) -> p s n", s=12)
        v_grp = sb("v_grp", [P, NT, G, 32])
        negmax = sb("negmax", [P, 2, 3, G])
        negm = sb("negm", [P, 3, G])
        negr = sb("negr", [P, 3, G])
        mparts = sb("mparts", [P, 2, 3, NPART * G], BF16)
        mrows = sb("mrows", [NPART * G, 2, 3 * P], BF16)
        two_bf16_ones = struct.unpack("<f", struct.pack("<I", 0x3F803F80))[0]
        qf = qstack[:, :, :].rearrange("p a n -> p (a n)").bitcast(F32)
        kf = kstack[:, :, :].rearrange("p a n -> p (a n)").bitcast(F32)
        rows = qf[:, 0:TT * ROW].rearrange("p (t n) -> p t n", t=TT)
        o_bat = kf[:, 0:2 * LP].rearrange("p (g n) -> p g n", g=2)
        w1_sb = kf[:, 1536:1536 + E * HID].rearrange("p (e n) -> p e n", e=E)
        w2_sb = kf[:, 3584:3584 + E * HID].rearrange("p (e c n) -> p e c n", e=E, c=HC)
        b1_bc = kf[:, 5632:5632 + E * HID].rearrange("p (e n) -> p e n", e=E)
        b2_bc = kf[:, 7680:7680 + E * O].rearrange("p (e n) -> p e n", e=E)
        on = kf[:, 8704:8704 + NT * O].rearrange("p (t n) -> p t n", t=NT)
        ont = kf[:, 9472:9472 + LP]
        rden = kf[:, 10240:10240 + NT * H]
        logits = kf[:, 10304:10304 + TT * E].rearrange("p (t e) -> p t e", e=E)
        bg_bc = sb("bg_bc", [P, E])
        wg_sb = sb("wg_sb", [P, E])
        def f_buf(at, n):
            return region[:, at:at + 4 * n].rearrange("p (u k n) -> p u k n", u=2, k=2)

        f_x, f_xt, f_h, f_ht = f_buf(0, O), f_buf(512, P), f_buf(1024, HID), f_buf(2048, HID)
        RING_F = 4
        f_y = region[:, 3072:3072 + RING_F * 2 * O].rearrange("p (u k n) -> p u k n", u=RING_F, k=2)
        f_r = qf[:, (TT + 1) * ROW:(TT + 1) * ROW + RING_F * 2 * (O + 1)].rearrange("p (u k n) -> p u k n", u=RING_F, k=2)
        r_max = sb("r_max", [P, TT])
        r_cand = sb("r_cand", [P, TT, E])
        r_hot = sb("r_hot", [P, TT, E])
        r_e8 = sb("r_e8", [P, E])
        r_valid = sb("r_valid", [P, TT])
        r_scan = sb("r_scan", [P, E, TT])
        r_excl = sb("r_excl", [P, E, TT])
        r_zero = sb("r_zero", [P, E * TT])
        r_cnt = sb("r_cnt", [P, E])
        r_lim = sb("r_lim", [P, TT + 1])
        r_more = sb("r_more", [P, E, TT + 1])
        r_tiles = sb("r_tiles", [P, E])
        r_upto = sb("r_upto", [P, E])
        r_off = sb("r_off", [P, E])
        r_pos = sb("r_pos", [P, TT, E])
        r_posf = sb("r_posf", [P, TT])
        r_posi = sb("r_posi", [P, TT], U32)
        r_tile_no = sb("r_tile_no", [P, FT])
        r_past = sb("r_past", [P, FT, E])
        r_expf = sb("r_expf", [P, FT])
        r_expi = sb("r_expi", [P, FT], I32)
        tri = sb("tri", [P, P])
        ones = sb("ones", [P, P])

        w_loaded, consts, x_pad = sem("w_loaded"), sem("consts"), sem("x_pad")
        w_t_ps, w_t_done = sem("w_t_ps"), sem("w_t_done")
        first_x_loaded, x_loaded, xt_ps, xt_done = sem("first_x_loaded"), sem("x_loaded"), sem("xt_ps"), sem("xt_done")
        conv_ps, h_done = sem("conv_ps"), sem("h_done")
        ln_chain, var_done, rstd_done, z_done = sem("ln_chain"), sem("var_done"), sem("rstd_done"), sem("z_done")
        zt_ps, zt_done = sem("zt_ps"), sem("zt_done")
        q_ps, k_ps, v_ps, v_done = sem("q_ps"), sem("k_ps"), sem("v_ps"), sem("v_done")
        hi_done, rest_done, mid_done, lo_done = sem("hi_done"), sem("rest_done"), sem("mid_done"), sem("lo_done")
        parts_stored, stack_loaded = sem("parts_stored"), sem("stack_loaded")
        hb_done = sem("hb_done")
        max_ps, max_done, msplit, msplit_chain = sem("max_ps"), sem("max_done"), sem("msplit"), sem("msplit_chain")
        mrow_ps, mrow_done = sem("mrow_ps"), sem("mrow_done")
        mrows_a, mrows_b = sem("mrows_a"), sem("mrows_b")
        score_ps, exp_done, pv_done, vgrp_done, o_done = (
            sem("score_ps"), sem("exp_done"), sem("pv_done"), sem("vgrp_done"), sem("o_done"))
        o_loaded, ot_ps, rden_done, on_done = sem("o_loaded"), sem("ot_ps"), sem("rden_done"), sem("on_done")
        ont_ps, ont_done, agg_ps, h2_done = sem("ont_ps"), sem("ont_done"), sem("agg_ps"), sem("h2_done")
        z2t_ps, z2t_done, log_ps, log_done = sem("z2t_ps"), sem("z2t_done"), sem("log_ps"), sem("log_done")
        ln2_chain, var2_done, rstd2_done, z2_done = sem("ln2_chain"), sem("var2_done"), sem("rstd2_done"), sem("z2_done")
        pow_chain, pow2_chain = sem("pow_chain"), sem("pow2_chain")
        parts_free = sem("parts_free")
        zc_done, wg_loaded, experts_loaded = sem("zc_done"), sem("wg_loaded"), sem("experts_loaded")
        r_chain, r_hot_done, rank_ps, pos_done, expert_done = (
            sem("r_chain"), sem("r_hot_done"), sem("rank_ps"), sem("pos_done"), sem("expert_done"))
        scattered, fxt_ps, fxt_done = sem("scattered"), sem("fxt_ps"), sem("fxt_done")
        fx_loaded = [sem(f"fx_loaded{u}") for u in range(2)]
        fr_loaded, out_stored = ([sem(f"{n}{u}") for u in range(RING_F)] for n in ("fr_loaded", "out_stored"))
        fh_ps, fh_done, fht_ps, fht_done = sem("fh_ps"), sem("fh_done"), sem("fht_ps"), sem("fht_done")
        fy_ps, fy_done = sem("fy_ps"), sem("fy_done")
        fy_chain = sem("fy_chain")
        turns = sem("turns")
        fill_done, filled, ids_done = sem("fill_done"), sem("filled"), sem("ids_done")
        krows_done, r_consts = sem("krows_done"), sem("r_consts")

        EXP_FREE, PV_FREE = 3, 3
        ONE_FREE = 1
        FY_FREE = 4
        assert NPAIR % RING_F == 0 and NPAIR > 2 * RING_F

        UNITS = NT * G
        X_STEP = {1: 7, 0: 17}
        SETS = 2 * NT
        PAIRS = G * SETS
        STACK = 16 * (len(Q_RUNS) + len(K_RUNS))
        HS = NT // 2
        HSTEPS = SETS
        NCONST = 11

        def krows(t):
            return P if t < NT - 1 else LAST

        def x_bank(half, first=False):
            return bank(4 if first else 4 + (2 * X_STEP[half] + 1) % 3)

        block = ctx.enter_context(nc.Block())

        def load_x(engine, b, loaded):
            for k, n in ((0, XLAST), (1, XLAST - 1)):
                engine.dma_start(x_in[:, 0:NT - 1, k * D:(k + 1) * D],
                                 x[b, k:k + (NT - 1) * P, :].rearrange("(t p) d -> p t d", p=P)).then_inc(loaded, 16)
                engine.dma_start(x_in[0:n, NT - 1, k * D:(k + 1) * D],
                                 x[b, k + (NT - 1) * P:T, :]).then_inc(loaded, 16)

        @block.sync
        def _(sp):
            sp.sem_inc(parts_free, ONE_FREE)
            sp.wait_ge(x_pad, 1)
            load_x(sp, 0, first_x_loaded)
            sp.dma_start(w_in[:, 0:CTX * D], tok_w[:, :]).then_inc(w_loaded, 16)
            sp.dma_start(w_in[:, 320:704].rearrange("p (a n) -> p a n", a=3),
                         w_qkv.rearrange("(a p) n -> p a n", p=P)).then_inc(w_loaded, 16)
            sp.dma_start(w_in[:, 704:832], w_agg[:, :]).then_inc(w_loaded, 16)
            sp.dma_start(tokb_bc[:], tok_b.partition_broadcast(P)).then_inc(w_loaded, 16)
            sp.dma_start(bagg_bc[:], b_agg.partition_broadcast(P)).then_inc(w_loaded, 16)
            sp.dma_start(wg_sb[:], wg[:, :]).then_inc(wg_loaded, 16)
            sp.dma_start(bg_bc[:], bg.partition_broadcast(P)).then_inc(wg_loaded, 16)

            with sp.Fori(0, B) as b:
                for a in range(2):
                    for c in range(NPART):
                        if c == 0:
                            sp.wait_ge(hi_done, 2 * b + a + 1)
                            sp.sem_inc(turns, 1)
                        elif c == 1:
                            sp.wait_ge(mid_done, 2 * b + a + 1)
                            sp.sem_inc(turns, 1)
                        else:
                            sp.wait_ge(lo_done, 2 * b + a + 1)
                            sp.sem_inc(turns, 1)
                        sp.dma_start(parts_dram[a, b, :, c * DH:(c + 1) * DH, :],
                                     parts[:, a, c, :]).then_inc(parts_stored, 16)
                sp.wait_ge(parts_stored, 16 * 2 * NPART * (b + 1))
                sp.sem_inc(parts_free, 1)
                for a, dst, runs in ((0, qstack, Q_RUNS), (1, kstack, K_RUNS)):
                    for slot, c, n in runs:
                        sp.dma_start(dst[slot * DH:(slot + n) * DH, bass.ds(b * H, H), :],
                                     parts_dram[a, b, :, c * DH:(c + n) * DH, :].rearrange("h r n -> r h n")
                                     ).then_inc(stack_loaded, 16)
                sp.wait_ge(stack_loaded, STACK * (b + 1))
                sp.sem_inc(turns, 1)

            def max_rows(half, grp, n_done):
                cols, s = ((0, 3 * P), mrows_a) if half == 0 else ((3 * P, L), mrows_b)
                sp.wait_ge(mrow_done, n_done)
                sp.sem_inc(turns, 1)
                for c in range(NPART):
                    sp.dma_start(qstack[KR + c:KR + c + 1, bass.ds(grp * G, G), cols[0]:cols[1]],
                                 mrows[c * G:(c + 1) * G, half, 0:cols[1] - cols[0]]).then_inc(s, 16)

            def fill_places(i):
                sp.dma_start(xs_dram[bass.ds(i * (FT // NG) * P, FT // NG * P), :].rearrange("(t p) n -> p t n", p=P),
                             fill.rearrange("p (a n) -> p a n", a=1).to_broadcast([P, FT // NG, ROW])).then_inc(filled, 16)

            def load_o(b):
                sp.dma_start(o_bat[:, :, :], o_all[:, bass.ds(b * GB, GB), :]).then_inc(o_loaded, 16)

            EB = E // B

            def load_experts(i):
                e = bass.ds(i * EB, EB)
                sp.dma_start(w1_sb[:, e, :], w1[e, :, :].rearrange("e d n -> d e n")).then_inc(experts_loaded, 16)
                for c in range(HC):
                    sp.dma_start(w2_sb[:, e, c, :], w2[e, c * P:(c + 1) * P, :].rearrange("e p n -> p e n")
                                 ).then_inc(experts_loaded, 16)
                sp.dma_start(b1_bc[:, e, :], b1[e, :].partition_broadcast(P)).then_inc(experts_loaded, 16)
                sp.dma_start(b2_bc[:, e, :], b2[e, :].partition_broadcast(P)).then_inc(experts_loaded, 16)

            max_rows(0, 0, 1)
            sp.wait_ge(fill_done, 2)
            with sp.Fori(0, NG - 1) as g:
                max_rows(1, g, 2 * g + 2)
                max_rows(0, g + 1, 2 * g + 3)
                fill_places(g)
            sp.wait_ge(pv_done, PV_FREE + SETS * (NG - 1))
            load_o(0)
            max_rows(1, NG - 1, 2 * NG)
            with sp.Fori(1, B) as b:
                sp.wait_ge(ot_ps, b)
                sp.sem_inc(turns, 1)
                sp.wait_ge(o_done, ONE_FREE + 2 * GB * (b + 1))
                sp.sem_inc(turns, 1)
                load_o(b)
                load_experts(b - 1)
            load_experts(B - 1)
            fill_places(NG - 1)

            def load_pair(q, u, m):
                sp.dma_start(f_x[:, u, :, :], xs_dram[bass.ds(q * 2 * P, 2 * P), 0:O].rearrange("(k p) n -> p k n", p=P)
                             ).then_inc(fx_loaded[u], 16)

            def load_residual(q, u, m, free=True):
                if free:
                    sp.wait_ge(out_stored[u], 32 * m)
                    sp.sem_inc(turns, 1)
                sp.dma_start(f_r[:, u, :, :], xs_dram[bass.ds(q * 2 * P, 2 * P), O:ROW].rearrange("(k p) n -> p k n", p=P)
                             ).then_inc(fr_loaded[u], 16)

            def next_pair(q, u, m):
                sp.wait_ge(fxt_ps, q - 1)
                sp.sem_inc(turns, 1)
                load_pair(q, u, m)

            sp.wait_ge(scattered, 16 * TT)
            load_pair(0, 0, 0)
            load_pair(1, 1, 0)
            for u in range(RING_F):
                load_residual(u, u, 0, free=False)
            AHEAD = 3
            for q in range(2, RING_F + AHEAD):
                next_pair(q, q % 2, q // 2)
            with sp.Fori(1, NPAIR // RING_F - 1) as j:
                for u in range(RING_F):
                    next_pair(RING_F * j + u + AHEAD, (u + AHEAD) % 2, RING_F // 2 * j + (u + AHEAD) // 2)
                    load_residual(RING_F * j + u, u, j)
            next_pair(NPAIR - 1, 1, NPAIR // 2 - 1)
            for u in range(RING_F):
                load_residual(NPAIR - RING_F + u, u, NPAIR // RING_F - 1)
            for u in range(RING_F):
                sp.wait_ge(out_stored[u], 32 * (NPAIR // RING_F))

        @block.gpsimd
        def _(pool):
            nc.gpsimd.memset(ident[:], 0.0).then_inc(consts, 1)
            pool.wait_ge(consts, 1)
            nc.gpsimd.affine_select(out=ident[:], in_=ident[:], compare_op=ALU.not_equal, fill=1.0, base=0,
                                    pattern=[[-1, P]], channel_multiplier=1).then_inc(consts, 1)
            nc.gpsimd.memset(xt[:, LP:LP + 8], 0.0).then_inc(consts, 1)
            nc.gpsimd.memset(minus_half[:], -0.5).then_inc(consts, 1)
            nc.gpsimd.memset(ones[:], 1.0).then_inc(consts, 1)
            nc.gpsimd.memset(r_zero[:], 0.0).then_inc(consts, 1)
            nc.gpsimd.memset(v_grp[:], 0.0).then_inc(consts, 1)
            nc.gpsimd.memset(negmax[:], 0.0).then_inc(consts, 1)
            pool.wait_ge(consts, 8)
            nc.gpsimd.tensor_copy(identb[:], ident[:]).then_inc(consts, 1)
            nc.gpsimd.memset(v_grp[:, :, :, DH:DH + 1], 1.0).then_inc(consts, 1)
            nc.gpsimd.memset(o_all[:, :, L:LP], 1.0).then_inc(consts, 1)

            def deviations(b, var, chain, done):
                pool.wait_ge(var, b + 1)
                nc.gpsimd.tensor_tensor(rstd[:], veps[:], minus_half[:], ALU.pow).then_inc(chain, 1)
                pool.wait_ge(chain, b + 1)
                nc.gpsimd.tensor_tensor(nmr[:], nmean[:], rstd[:], ALU.mult).then_inc(done, 1)

            def residual_bias(b):
                pool.wait_ge(w_loaded, 16 * 5)
                pool.wait_ge(z_done, b + 1)
                h = hres[:, bass.ds(b * NT, NT), :]
                nc.gpsimd.tensor_tensor(h, h, bagg_bc[:].rearrange("p (a n) -> p a n", a=1).to_broadcast([P, NT, O]),
                                        ALU.add).then_inc(hb_done, 1)

            def next_x(b):
                pool.wait_ge(xt_ps, b)
                pool.sem_inc(turns, 1)
                load_x(pool, b, x_loaded)

            next_x(1)
            deviations(0, var_done, pow_chain, rstd_done)
            residual_bias(0)
            with pool.Fori(1, B - 1) as b:
                next_x(b + 1)
                deviations(b, var_done, pow_chain, rstd_done)
                residual_bias(b)
            deviations(B - 1, var_done, pow_chain, rstd_done)
            residual_bias(B - 1)

            nc.gpsimd.iota(r_e8[:], pattern=[[-1, E]], base=E, channel_multiplier=0,
                           allow_small_or_imprecise_dtypes=True).then_inc(r_consts, 1)
            nc.gpsimd.iota(r_lim[:], pattern=[[P, TT + 1]], base=0, channel_multiplier=0,
                           allow_small_or_imprecise_dtypes=True).then_inc(r_consts, 1)
            nc.gpsimd.iota(r_tile_no[:], pattern=[[1, FT]], base=0, channel_multiplier=0,
                           allow_small_or_imprecise_dtypes=True).then_inc(r_consts, 1)
            nc.gpsimd.memset(r_valid[:], 1.0).then_inc(r_consts, 1)
            pool.wait_ge(r_consts, 4)
            nc.gpsimd.affine_select(out=r_valid[:, NT - 1:TT:NT], in_=r_valid[:, NT - 1:TT:NT], compare_op=ALU.is_ge,
                                    fill=0.0, base=LAST - 1, pattern=[[0, B]],
                                    channel_multiplier=-1).then_inc(r_consts, 1)
            nc.gpsimd.affine_select(out=tri[:], in_=ones[:], compare_op=ALU.is_gt, fill=0.0, base=0,
                                    pattern=[[1, P]], channel_multiplier=-1).then_inc(r_consts, 1)

            pool.wait_ge(xt_ps, B)
            nc.gpsimd.memset(fill[:, 0:ROW - 1], 0.0).then_inc(fill_done, 1)
            nc.gpsimd.memset(fill[:, ROW - 1:ROW].bitcast(I32), B * L).then_inc(fill_done, 1)

            def split_maxima(half, grp, idx):
                pool.wait_ge(max_done, UNITS * grp + HS * G * (half + 1))
                pool.sem_inc(turns, 1)
                src, dst = negmax[:, half, :, :], mparts[:, half, :, :]
                nc.gpsimd.tensor_copy(dst[:, :, 0:G], src).then_inc(msplit_chain, 1)
                pool.wait_ge(msplit_chain, 3 * idx + 1)
                nc.gpsimd.tensor_tensor(negr[:], src, dst[:, :, 0:G], ALU.subtract).then_inc(msplit_chain, 1)
                pool.wait_ge(msplit_chain, 3 * idx + 2)
                pool.sem_inc(turns, 1)
                nc.gpsimd.tensor_copy(dst[:, :, G:2 * G], negr[:]).then_inc(msplit_chain, 1)
                pool.wait_ge(msplit_chain, 3 * idx + 3)
                nc.gpsimd.tensor_tensor(dst[:, :, 2 * G:3 * G], negr[:], dst[:, :, G:2 * G],
                                        ALU.subtract).then_inc(msplit, 1)

            def copy_values(grp, t):
                nc.gpsimd.tensor_copy(v_grp[:, t, :, 0:DH],
                                      v_all[:, grp, t, :].rearrange("p (h d) -> p h d", h=G)).then_inc(vgrp_done, 1)

            pool.wait_ge(v_done, 1)
            for t in range(NT):
                copy_values(0, t)
            split_maxima(0, 0, 0)
            split_maxima(1, 0, 1)
            with pool.Fori(0, NG - 1) as g:
                split_maxima(0, g + 1, 2 * g + 2)
                for t in range(NT):
                    if t == NT - 2:
                        split_maxima(1, g + 1, 2 * g + 3)
                    pool.wait_ge(pv_done, SETS * g + PV_FREE + NT + t + 1)
                    pool.sem_inc(turns, 1)
                    copy_values(g + 1, t)

            pool.wait_ge(pv_done, PV_FREE + SETS * (NG - 1))
            nc.gpsimd.iota(rows[:, :, ROW - 1].bitcast(I32), pattern=[[L, B], [P, NT]], base=0,
                           channel_multiplier=1).then_inc(ids_done, 1)

            def copy_z(b):
                nc.gpsimd.tensor_copy(rows[:, bass.ds(b * NT, NT), 0:O], z[:]).then_inc(zc_done, 1)

            pool.sem_inc(zc_done, ONE_FREE)
            deviations(0, var2_done, pow2_chain, rstd2_done)
            with pool.Fori(0, B - 1) as b:
                pool.wait_ge(z2_done, b + 1)
                pool.sem_inc(turns, 1)
                deviations(b + 1, var2_done, pow2_chain, rstd2_done)
                copy_z(b)
            pool.wait_ge(z2_done, B)
            copy_z(B - 1)

            pool.wait_ge(zc_done, ONE_FREE + B)
            pool.wait_ge(ids_done, 1)
            pool.wait_ge(filled, 16 * NG)
            pool.wait_ge(pos_done, 1)
            for t in range(TT):
                n = krows(t % NT)
                pool.indirect_dma_start(out=xs_dram[:, :],
                                        out_offset=bass.IndirectOffsetOnAxis(ap=r_posi[0:n, t:t + 1], axis=0),
                                        in_=rows[0:n, t, :], in_offset=None).then_inc(scattered, 16)
            def scatter_out(q, u):
                for k in range(2):
                    pool.wait_ge(fy_done, FY_FREE + 2 * q + k + 1)
                    pool.sem_inc(turns, 1)
                    pool.indirect_dma_start(out=out.rearrange("b l n -> (b l) n"),
                                            out_offset=bass.IndirectOffsetOnAxis(
                                                ap=f_r[:, u, k, O:O + 1].bitcast(U32), axis=0),
                                            in_=f_y[:, u, k, :], in_offset=None, bounds_check=B * L - 1,
                                            oob_is_err=False).then_inc(out_stored[u], 16)

            with pool.Fori(0, NPAIR // RING_F) as j:
                for u in range(RING_F):
                    scatter_out(RING_F * j + u, u)

        @block.scalar
        def _(act):
            def copy_xt(b):
                act.wait_ge(xt_ps, b + 1)
                nc.scalar.copy(xt[:, 0:LP], ps[:, 0:LP]).then_inc(xt_done, 1)

            def normalise(b, src, ready, done):
                act.wait_ge(ready, b + 1)
                for t in range(NT):
                    last = nc.scalar.activation(z[:, t, :], src(b * NT + t), ACT.Identity,
                                                bias=nmr[:, t:t + 1], scale=rstd[:, t:t + 1])
                last.then_inc(done, 1)

            def copy_zt(b):
                act.wait_ge(zt_ps, b + 1)
                nc.scalar.copy(zt[:], ps[:, 4 * 512:4 * 512 + LP]).then_inc(zt_done, 1)

            def qkv_copies(b):
                act.wait_ge(parts_free, b + 1)
                for a, (ready, first) in enumerate(((q_ps, 6), (k_ps, 0))):
                    act.wait_ge(ready, b + 1)
                    nc.scalar.copy(parts[:, a, 0, :].rearrange("p (c n) -> p c n", c=2),
                                   ps[:, first * 512:(first + 2) * 512].rearrange("p (c n) -> p c n", c=2)[:, :, 0:HALF]
                                   ).then_inc(hi_done, 1)
                act.wait_ge(v_ps, b + 1)
                nc.scalar.copy(v_all[:, bass.ds(b * GB, GB), :, :].rearrange("p g t n -> p t g n"),
                               ps[:, 4 * 512:4 * 512 + LP].rearrange("p (t g n) -> p t g n", t=NT, g=GB)
                               ).then_inc(v_done, 1)

            def second_thirds(b):
                for a in range(2):
                    act.wait_ge(rest_done, 2 * b + a + 1)
                    nc.scalar.copy(parts[:, a, 1, :], rest[:, a, :]).then_inc(mid_done, 1)

            def h_tile(t):
                return hres[:, t, :]

            act.wait_ge(consts, NCONST)
            copy_xt(0)
            act.wait_ge(w_t_ps, 1)
            nc.scalar.copy(w_conv[:, 0:2 * P], bank(2, 2 * P)).then_inc(w_t_done, 1)
            nc.scalar.copy(w_conv[0:D, 2 * P:3 * P], bank(2)[0:D, 2 * P:3 * P]).then_inc(w_t_done, 1)
            nc.scalar.copy(w_proj[:], bank(3)).then_inc(w_t_done, 1)
            normalise(0, h_tile, rstd_done, z_done)
            with act.Fori(0, B - 1) as b:
                copy_zt(b)
                copy_xt(b + 1)
                qkv_copies(b)
                normalise(b + 1, h_tile, rstd_done, z_done)
                second_thirds(b)
            copy_zt(B - 1)
            qkv_copies(B - 1)
            second_thirds(B - 1)

            act.sem_inc(exp_done, EXP_FREE)
            act.sem_inc(o_done, ONE_FREE)

            def copy_max_rows(half, idx, first=False):
                act.wait_ge(mrow_ps, idx + 1)
                nc.scalar.copy(mrows[:, half, :],
                               x_bank(half, first).bitcast(BF16)[0:NPART * G, 0:HS * P]).then_inc(mrow_done, 1)

            def exponentials(g, s, last=False):
                n = krows((s % HSTEPS) // 2)
                for a in range(2):
                    k = 2 * s + a
                    if k % G == 0:
                        act.wait_ge(pv_done, SETS * g + k // G + 1)
                    act.wait_ge(score_ps, PAIRS * g + k + 1)
                    nc.scalar.activation(probs[0:n, k % 12, :], ps[0:n, (4 + k % 3) * 512:(4 + k % 3) * 512 + HALF],
                                         ACT.Exp, scale=SCALE).then_inc(exp_done, 1)
                    if a == 0 and s == X_STEP[1]:
                        copy_max_rows(1, 2 * g + 1)
                    if a == 0 and s == X_STEP[0] and not last:
                        copy_max_rows(0, 2 * g + 2)
                if s == HSTEPS + 1:
                    copy_outputs(g, 0)

            def copy_outputs(g, half):
                act.wait_ge(pv_done, SETS * g + PV_FREE + NT * (half + 1))
                nc.scalar.copy(o_all[:, g, half * HALF:(half + 1) * HALF], bank(7, HALF)).then_inc(o_done, 1)

            copy_max_rows(0, 0, first=True)
            act.wait_ge(parts_free, B + 1)
            for s in range(2):
                exponentials(0, s)
            with act.Fori(0, NG - 1) as g:
                for s in range(2, UNITS):
                    exponentials(g, s)
                for s in range(2):
                    exponentials(g + 1, s)
                copy_outputs(g, 1)
            for s in range(2, UNITS):
                exponentials(NG - 1, s, last=True)
            copy_outputs(NG - 1, 1)

            def residual_tile(t):
                return rows[:, t, O:2 * O]

            with act.Fori(0, B) as b:
                act.wait_ge(zc_done, ONE_FREE + b)
                normalise(b, residual_tile, rstd2_done, z2_done)
                act.wait_ge(z2t_ps, b + 1)
                nc.scalar.copy(zt[:], ps[:, 4 * 512:4 * 512 + LP]).then_inc(z2t_done, 1)

            def copy_tokens(q, u):
                act.wait_ge(fxt_ps, q + 1)
                nc.scalar.copy(f_xt[:, u, :, :], bank(0, 2 * P).rearrange("p (k n) -> p k n", k=2)).then_inc(fxt_done, 1)

            def hidden(q, u):
                act.wait_ge(fht_ps, q + 1)
                nc.scalar.activation(f_ht[:, u, :, :].rearrange("p k n -> p (k n)"), bank(3), ACT.Relu).then_inc(fht_done, 1)

            copy_tokens(0, 0)
            copy_tokens(1, 1)
            copy_tokens(2, 0)
            hidden(0, 0)
            with act.Fori(0, NPAIR // 2 - 2) as j:
                copy_tokens(2 * j + 3, 1)
                hidden(2 * j + 1, 1)
                copy_tokens(2 * j + 4, 0)
                hidden(2 * j + 2, 0)
            copy_tokens(NPAIR - 1, 1)
            for q in range(NPAIR - 3, NPAIR):
                hidden(q, q % 2)

        @block.vector
        def _(dve):
            def ln_stats(b, src, chain, var):
                dve.sem_inc(turns, 1)
                for t in range(NT):
                    last = nc.vector.bn_stats(stats[:, t, :], src(b * NT + t))
                last.then_inc(chain, 1)
                dve.wait_ge(chain, 2 * b + 1)
                dve.sem_inc(turns, 1)
                for t in range(NT):
                    last = nc.vector.bn_aggr(mv[:, t, :], stats[:, t, :])
                last.then_inc(chain, 1)
                dve.wait_ge(chain, 2 * b + 2)
                nc.vector.tensor_scalar(veps[:], mv[:, :, 1], EPS, None, ALU.add)
                nc.vector.tensor_scalar(nmean[:], mv[:, :, 0], -1.0, None, ALU.mult).then_inc(var, 1)

            nc.vector.memset(x_in[:, NT - 1, :], 0.0).then_inc(x_pad, 1)
            def add_conv_bias(b):
                dve.wait_ge(conv_ps, b + 1)
                nc.vector.tensor_tensor(hres[:, bass.ds(b * NT, NT), :],
                                        ps[:, 2 * 512:2 * 512 + LP].rearrange("p (t n) -> p t n", t=NT),
                                        tokb_bc[:].rearrange("p (a n) -> p a n", a=1).to_broadcast([P, NT, O]),
                                        ALU.add).then_inc(h_done, 1)

                dve.wait_ge(h_done, b + 1)
                ln_stats(b, lambda t: hres[:, t, :], ln_chain, var_done)

            def thirds(b):
                for a, first in enumerate((6, 0)):
                    dve.wait_ge(hi_done, 2 * b + a + 1)
                    nc.vector.tensor_tensor(rest[:, a, :].rearrange("p (c n) -> p c n", c=2),
                                            ps[:, first * 512:(first + 2) * 512].rearrange("p (c n) -> p c n", c=2)[:, :, 0:HALF],
                                            parts[:, a, 0, :].rearrange("p (c n) -> p c n", c=2),
                                            ALU.subtract).then_inc(rest_done, 1)
                for a in range(2):
                    dve.wait_ge(mid_done, 2 * b + a + 1)
                    nc.vector.tensor_tensor(parts[:, a, 2, :], rest[:, a, :], parts[:, a, 1, :],
                                            ALU.subtract).then_inc(lo_done, 1)

            dve.wait_ge(w_loaded, 16 * 5)
            add_conv_bias(0)
            nc.vector.memset(kf[KR:KR + NPART, :], two_bf16_ones).then_inc(krows_done, 1)
            with dve.Fori(0, B - 1) as b:
                add_conv_bias(b + 1)
                thirds(b)
            thirds(B - 1)

            def maxima(grp):
                for s in range(UNITS):
                    t, h = s // G, s % G
                    first = 2 * (s % 2)
                    n = krows(t)
                    dve.wait_ge(max_ps, UNITS * grp + s + 1)
                    nc.vector.tensor_reduce(negmax[0:n, t // HS, t % HS, h:h + 1],
                                            ps[0:n, first * 512:(first + 2) * 512].rearrange("p (c n) -> p c n", c=2)[:, :, 0:HALF],
                                            axis=AX.XY, op=ALU.max, negate=True).then_inc(max_done, 1)

            dve.wait_ge(consts, NCONST)
            maxima(0)
            with dve.Fori(0, NG - 1) as g:
                maxima(g + 1)

            def normalise(b):
                dve.wait_ge(ot_ps, b + 1)
                heads = ps[:, 0:NT * H * 32].rearrange("p (a n) -> p a n", n=32)
                nc.vector.reciprocal(rden, heads[:, :, DH]).then_inc(rden_done, 1)
                dve.wait_ge(rden_done, b + 1)
                nc.vector.tensor_tensor(on.rearrange("p t (h d) -> p (t h) d", d=DH), heads[:, :, 0:DH],
                                        rden.rearrange("p (a n) -> p a n", n=1).to_broadcast([P, NT * H, DH]),
                                        ALU.mult).then_inc(on_done, 1)

            def copy_ont(b):
                dve.wait_ge(ont_ps, b + 1)
                nc.vector.tensor_copy(ont, ps[:, 0:LP]).then_inc(ont_done, 1)

            def add_residual(b):
                dve.wait_ge(agg_ps, b + 1)
                h = hres[:, bass.ds(b * NT, NT), :]
                nc.vector.tensor_tensor(rows[:, bass.ds(b * NT, NT), O:2 * O], 
                                        ps[:, 2 * 512:2 * 512 + LP].rearrange("p (t n) -> p t n", t=NT), h,
                                        ALU.add).then_inc(h2_done, 1)

            def router_logits(b):
                dve.wait_ge(log_ps, b + 1)
                nc.vector.tensor_tensor(logits[:, bass.ds(b * NT, NT), :],
                                        bank(6, NT * E).rearrange("p (t e) -> p t e", e=E),
                                        bg_bc[:].rearrange("p (a e) -> p a e", a=1).to_broadcast([P, NT, E]),
                                        ALU.add).then_inc(log_done, 1)

            def layer_norm_2(b):
                dve.wait_ge(h2_done, b + 1)
                ln_stats(b, lambda t: rows[:, t, O:2 * O], ln2_chain, var2_done)

            dve.wait_ge(hb_done, B)
            dve.wait_ge(wg_loaded, 16 * 2)
            for b in range(2):
                normalise(b)
                copy_ont(b)
                add_residual(b)
                if b == 1:
                    dve.wait_ge(rstd2_done, 1)
                layer_norm_2(b)
            with dve.Fori(0, B - 2) as b:
                normalise(b + 2)
                copy_ont(b + 2)
                router_logits(b)
                add_residual(b + 2)
                dve.wait_ge(rstd2_done, b + 2)
                layer_norm_2(b + 2)
            for b in range(B - 2, B):
                router_logits(b)

            chain = [0]

            def link(ins):
                chain[0] += 1
                ins.then_inc(r_chain, 1)
                dve.wait_ge(r_chain, chain[0])

            def over_e(ap, n):
                return ap.rearrange("p (n a) -> p n a", a=1).to_broadcast([P, n, E])

            dve.wait_ge(r_consts, 6)
            dve.wait_ge(log_done, B)
            link(nc.vector.tensor_reduce(r_max[:], logits, axis=AX.X, op=ALU.max))
            link(nc.vector.tensor_tensor(r_cand[:], logits, over_e(r_max[:], TT), ALU.is_equal))
            link(nc.vector.tensor_tensor(r_cand[:], r_cand[:], r_e8[:].rearrange("p (a e) -> p a e", a=1)
                                         .to_broadcast([P, TT, E]), ALU.mult))
            link(nc.vector.tensor_reduce(r_max[:], r_cand[:], axis=AX.X, op=ALU.max))
            link(nc.vector.tensor_tensor(r_hot[:], r_cand[:], over_e(r_max[:], TT), ALU.is_equal))
            nc.vector.tensor_tensor(r_hot[:], r_hot[:], over_e(r_valid[:], TT), ALU.mult).then_inc(r_hot_done, 1)
            dve.wait_ge(rank_ps, 1)
            totals = bank(1, TT * E).rearrange("p (t e) -> p e t", e=E)
            link(nc.vector.tensor_copy(r_excl[:], totals))
            link(nc.vector.tensor_reduce(r_cnt[:], r_excl[:], axis=AX.X, op=ALU.add))
            link(nc.vector.tensor_tensor(r_more[:], r_cnt[:].rearrange("p (e a) -> p e a", a=1).to_broadcast([P, E, TT + 1]),
                                         r_lim[:].rearrange("p (a n) -> p a n", a=1).to_broadcast([P, E, TT + 1]), ALU.is_gt))
            link(nc.vector.tensor_reduce(r_tiles[:], r_more[:], axis=AX.X, op=ALU.add))
            link(nc.vector.tensor_tensor_scan(out=r_upto[:], data0=r_zero[:, 0:E], data1=r_tiles[:], initial=0.0,
                                              op0=ALU.add, op1=ALU.add))
            flat = r_excl[:].rearrange("p e t -> p (e t)")
            link(nc.vector.tensor_tensor_scan(out=r_scan[:].rearrange("p e t -> p (e t)"), data0=r_zero[:], data1=flat,
                                              initial=0.0, op0=ALU.add, op1=ALU.add))
            link(nc.vector.tensor_tensor(r_excl[:], r_scan[:], r_excl[:], ALU.subtract))
            link(nc.vector.tensor_tensor(r_off[:], r_upto[:], r_tiles[:], ALU.subtract))
            link(nc.vector.scalar_tensor_tensor(out=r_off[:], in0=r_off[:], scalar=float(P), in1=r_excl[:, :, 0],
                                                op0=ALU.mult, op1=ALU.subtract))
            link(nc.vector.tensor_tensor(r_pos[:], bank(0, TT * E).rearrange("p (t e) -> p t e", e=E),
                                         r_excl[:].rearrange("p e t -> p t e"), ALU.add))
            link(nc.vector.tensor_tensor(r_pos[:], r_pos[:], r_off[:].rearrange("p (a e) -> p a e", a=1)
                                         .to_broadcast([P, TT, E]), ALU.add))
            link(nc.vector.tensor_tensor(r_pos[:], r_pos[:], r_hot[:], ALU.mult))
            link(nc.vector.tensor_reduce(r_posf[:], r_pos[:], axis=AX.X, op=ALU.add))
            nc.vector.tensor_copy(r_posi[:], r_posf[:]).then_inc(pos_done, 1)
            link(nc.vector.tensor_tensor(r_past[:], over_e(r_tile_no[:], FT),
                                         r_upto[:].rearrange("p (a e) -> p a e", a=1).to_broadcast([P, FT, E]), ALU.is_ge))
            link(nc.vector.tensor_reduce(r_expf[:], r_past[:], axis=AX.X, op=ALU.add))
            link(nc.vector.tensor_scalar(r_expf[:], r_expf[:], float(E - 1), None, ALU.min))
            nc.vector.tensor_copy(r_expi[:], r_expf[:]).then_inc(expert_done, 1)
            dve.wait_ge(expert_done, 1)

            def experts(q):
                return [dve.value_load(r_expi[0:1, bass.ds(q * 2 + k, 1)], min_val=0, max_val=E - 1) for k in range(2)]

            def hidden_bias(q, u):
                e = experts(q)
                dve.wait_ge(fh_ps, q + 1)
                for k in range(2):
                    nc.vector.tensor_tensor(f_h[:, u, k, :], bank(1 + u)[:, k * HID:(k + 1) * HID],
                                            b1_bc[:, e[k], :], ALU.add).then_inc(fh_done, 1)

            def results(q, u, m):
                e = experts(q)
                dve.wait_ge(fr_loaded[u], 16 * (m + 1))
                for k in range(2):
                    last = nc.vector.tensor_tensor(f_r[:, u, k, 0:O], f_r[:, u, k, 0:O], b2_bc[:, e[k], :], ALU.add)
                last.then_inc(fy_chain, 1)
                dve.wait_ge(fy_chain, q + 1)
                dve.wait_ge(fy_ps, q + 1)
                for k in range(2):
                    nc.vector.tensor_tensor(f_y[:, u, k, :], bank(4 + u % 2)[:, k * O:(k + 1) * O],
                                            f_r[:, u, k, 0:O], ALU.add).then_inc(fy_done, 1)

            dve.wait_ge(experts_loaded, 16 * 5 * B)
            dve.sem_inc(fy_done, FY_FREE)
            hidden_bias(0, 0)
            hidden_bias(1, 1)
            with dve.Fori(0, NPAIR // RING_F - 1) as j:
                for u in range(RING_F):
                    hidden_bias(RING_F * j + u + 2, u % 2)
                    results(RING_F * j + u, u, j)
            for q in range(NPAIR - RING_F, NPAIR):
                if q + 2 < NPAIR:
                    hidden_bias(q + 2, q % 2)
                results(q, q % RING_F, NPAIR // RING_F - 1)

        @block.tensor
        def _(pe):
            def transpose_weights():
                pe.wait_ge(w_loaded, 16 * 5)
                for c in range(3):
                    w = min(P, CTX * D - c * P)
                    nc.tensor.transpose(bank(2)[0:w, c * P:(c + 1) * P], w_in[:, c * P:c * P + w], ident[:])
                for c in range(4):
                    last = nc.tensor.transpose(bank(3)[:, c * P:(c + 1) * P], w_in[:, 320 + c * P:320 + (c + 1) * P],
                                               ident[:])
                last.then_inc(w_t_ps, 1)
                pe.wait_ge(w_t_done, 3)

            def transpose_x(b, first=False):
                if first:
                    pe.wait_ge(first_x_loaded, 16 * 4)
                else:
                    pe.wait_ge(x_loaded, 16 * 4 * b)
                for t in range(NT):
                    last = nc.tensor.transpose(ps[:, t * P:(t + 1) * P], x_in[:, t, :], ident[:])
                last.then_inc(xt_ps, 1)

            def convolve(b, first=False):
                pe.wait_ge(xt_done, b + 1)
                if not first:
                    pe.wait_ge(h_done, b)
                for t in range(NT):
                    dst = ps[:, 2 * 512 + t * P:2 * 512 + (t + 1) * P]
                    nc.tensor.matmul(dst, xt[:, t * P:(t + 1) * P], w_conv[:, 0:P], start=True, stop=False)
                    nc.tensor.matmul(dst, xt[:, t * P + 2:(t + 1) * P + 2], w_conv[:, P:2 * P], start=False, stop=False)
                    last = nc.tensor.matmul(dst, xt[0:D, t * P + 4:(t + 1) * P + 4], w_conv[0:D, 2 * P:3 * P],
                                            start=False, stop=True)
                last.then_inc(conv_ps, 1)

            def transpose_z(b):
                pe.wait_ge(z_done, b + 1)
                for t in range(NT):
                    last = nc.tensor.transpose(ps[:, 4 * 512 + t * P:4 * 512 + (t + 1) * P], z[:, t, :], ident[:])
                last.then_inc(zt_ps, 1)

            def project(b):
                pe.wait_ge(zt_done, b + 1)
                for a, (done, first) in enumerate(((q_ps, 6), (k_ps, 0))):
                    for c in range(2):
                        last = nc.tensor.matmul(bank(first + c, HALF), w_proj[:, a * P:(a + 1) * P],
                                                zt[:, c * HALF:(c + 1) * HALF], start=True, stop=True)
                    last.then_inc(done, 1)
                for t in range(NT):
                    last = nc.tensor.matmul(ps[:, 4 * 512 + t * P:4 * 512 + (t + 1) * P], zt[:, t * P:(t + 1) * P],
                                            w_proj[:, 2 * P:3 * P], start=True, stop=True)
                last.then_inc(v_ps, 1)

            pe.wait_ge(consts, NCONST)
            transpose_x(0, first=True)
            transpose_weights()
            convolve(0, first=True)
            with pe.Fori(0, B - 1) as b:
                transpose_z(b)
                transpose_x(b + 1)
                convolve(b + 1)
                project(b)
                pe.wait_ge(v_done, b + 1)
                pe.wait_ge(rest_done, 2 * b + 2)
            transpose_z(B - 1)
            project(B - 1)

            def score_unit(s, grp, first=False):
                t, head = s // G, grp * G + s % G
                if not (first and s < 2):
                    pe.wait_ge(max_done, UNITS * grp + s - 1)
                n = krows(t)
                for c in range(2):
                    last = nc.tensor.matmul(ps[0:n, (2 * (s % 2) + c) * 512:(2 * (s % 2) + c) * 512 + HALF],
                                            qstack[0:KR, head, t * P:t * P + n],
                                            kstack[0:KR, head, c * HALF:(c + 1) * HALF], start=True, stop=True)
                last.then_inc(max_ps, 1)

            def transpose_maxima(half, g, first=False):
                pe.wait_ge(msplit, 2 * g + (2 if half else 3))
                if not first:
                    pe.wait_ge(exp_done, PAIRS * g + 2 * X_STEP[half] + 2)
                for t in range(HS):
                    last = nc.tensor.transpose(x_bank(half, first).bitcast(BF16)[0:NPART * G, t * P:(t + 1) * P],
                                               mparts[:, half, t, :], identb[:])
                last.then_inc(mrow_ps, 1)

            def transposed_scores(g, k):
                half, t, head = k // (2 * HSTEPS), k % (2 * HSTEPS) // G, g * G + k % G
                n = krows(t)
                if k == 0:
                    pe.wait_ge(mrows_a, 16 * NPART * (g + 1))
                if k == 2 * HSTEPS:
                    pe.wait_ge(mrows_b, 16 * NPART * (g + 1))
                pe.wait_ge(exp_done, PAIRS * g + k + 1)
                nc.tensor.matmul(ps[0:n, (4 + k % 3) * 512:(4 + k % 3) * 512 + HALF],
                                 kstack[0:KR + NPART, head, t * P:t * P + n],
                                 qstack[0:KR + NPART, head, half * HALF:(half + 1) * HALF],
                                 start=True, stop=True).then_inc(score_ps, 1)

            def value_products(g, n):
                half, t = n // NT, n % NT
                rows = krows(t)
                pe.wait_ge(exp_done, PAIRS * g + G * (n + 1) + EXP_FREE)
                if half == 0:
                    pe.wait_ge(vgrp_done, NT * g + t + 1)
                if t == 0:
                    pe.wait_ge(o_done, 2 * g + half + 1)
                for h in range(G):
                    last = nc.tensor.matmul(ps[32 * h:32 * (h + 1), 7 * 512:7 * 512 + HALF], v_grp[0:rows, t, h, :],
                                            probs[0:rows, (G * n + h) % 12, :], start=(t == 0), stop=(t == NT - 1))
                last.then_inc(pv_done, 1)

            def step(g, s, last=False, before=None):
                transposed_scores(g, 2 * s)
                if s == X_STEP[1]:
                    transpose_maxima(1, g)
                if s == X_STEP[0] and not last:
                    transpose_maxima(0, g)
                if s % 2 == 1 and s > 1:
                    value_products(g, (s - 1) // 2 - 1)
                if s == 1 and before is not None:
                    value_products(before, SETS - 1)
                if s == X_STEP[1]:
                    pe.wait_ge(mrow_done, 2 * g + 2)
                if s == X_STEP[0] and not last:
                    pe.wait_ge(mrow_done, 2 * g + 3)
                transposed_scores(g, 2 * s + 1)

            slot_reg, next_reg = pe.alloc_register("slot"), pe.alloc_register("next_slot")
            pe.sem_inc(pv_done, PV_FREE)
            pe.wait_ge(stack_loaded, STACK)
            pe.wait_ge(rest_done, 2 * B)
            pe.wait_ge(v_done, B)
            for s in range(UNITS - 2):
                score_unit(s, 0, first=True)
                if s == UNITS - 8:
                    transpose_maxima(0, -1, first=True)
            pe.wait_ge(stack_loaded, STACK * B)
            pe.wait_ge(krows_done, 1)
            pe.wait_ge(lo_done, 2 * B)
            for s in range(2):
                step(0, s)
                score_unit(UNITS - 2 + s, 0)
            with pe.Fori(0, NG - 1) as g:
                for s in range(2, HSTEPS):
                    step(g, s)
                    score_unit(s - 2, g + 1)
                pe.reg_mov(slot_reg, g)
                g_again = pe.snap(slot_reg, min_val=0, max_val=NG - 2)
                for s in range(HSTEPS, UNITS):
                    step(g_again, s)
                    score_unit(s - 2, g_again + 1)
                pe.reg_mov(next_reg, g_again + 1)
                g_next = pe.snap(next_reg, min_val=1, max_val=NG - 1)
                for s in range(2):
                    step(g_next, s, before=g_again)
                    score_unit(UNITS - 2 + s, g_next)

            def transpose_o(b, first=False):
                if not first:
                    pe.wait_ge(h2_done, b)
                pe.wait_ge(o_loaded, 16 * (b + 1))
                for t in range(NT):
                    for g in range(GB):
                        last = nc.tensor.transpose(ps[:, t * 256 + g * P:t * 256 + (g + 1) * P],
                                                   o_bat[:, g, t * P:(t + 1) * P], ident[:])
                last.then_inc(ot_ps, 1)

            def transpose_on(b):
                pe.wait_ge(on_done, b + 1)
                for t in range(NT):
                    last = nc.tensor.transpose(ps[:, t * P:(t + 1) * P], on[:, t, :], ident[:])
                last.then_inc(ont_ps, 1)

            def output_projection(b):
                pe.wait_ge(ont_done, b + 1)
                for t in range(NT):
                    last = nc.tensor.matmul(ps[:, 2 * 512 + t * P:2 * 512 + (t + 1) * P], ont[:, t * P:(t + 1) * P],
                                            w_proj[:, 3 * P:4 * P], start=True, stop=True)
                last.then_inc(agg_ps, 1)

            def transpose_z2(b):
                pe.wait_ge(z2_done, b + 1)
                for t in range(NT):
                    last = nc.tensor.transpose(ps[:, 4 * 512 + t * P:4 * 512 + (t + 1) * P], z[:, t, :], ident[:])
                last.then_inc(z2t_ps, 1)

            def router(b):
                pe.wait_ge(z2t_done, b + 1)
                for t in range(NT):
                    last = nc.tensor.matmul(bank(6)[:, t * E:(t + 1) * E], zt[:, t * P:(t + 1) * P], wg_sb[:],
                                            start=True, stop=True)
                last.then_inc(log_ps, 1)

            C_STEPS = {4: (transpose_o, 0), 7: (transpose_on, 0), 9: (output_projection, 0),
                       13: (transpose_o, 1), 16: (transpose_on, 1), 18: (output_projection, 1)}
            for s in range(2, UNITS):
                step(NG - 1, s, last=True)
                if s in C_STEPS:
                    part, b = C_STEPS[s]
                    if s == 4:
                        pe.wait_ge(max_done, UNITS * NG)
                        part(b, first=True)
                    else:
                        part(b)
            value_products(NG - 1, SETS - 1)
            pe.wait_ge(o_done, ONE_FREE + 2 * NG)
            with pe.Fori(0, B - 2) as b:
                transpose_o(b + 2)
                transpose_z2(b)
                transpose_on(b + 2)
                router(b)
                output_projection(b + 2)
            for b in range(B - 2, B):
                transpose_z2(b)
                pe.wait_ge(log_done, b)
                router(b)

            pe.wait_ge(r_hot_done, 1)
            hot = r_hot[:].rearrange("p t e -> p (t e)")
            nc.tensor.matmul(bank(0, TT * E), tri[:], hot, start=True, stop=True)
            nc.tensor.matmul(bank(1, TT * E), ones[:], hot, start=True, stop=True).then_inc(rank_ps, 1)
            pe.wait_ge(expert_done, 1)
            pe.wait_ge(experts_loaded, 16 * 5 * B)

            def transpose_tokens(q, u, m, first=False):
                if not first:
                    pe.wait_ge(fxt_done, q)
                pe.wait_ge(fx_loaded[u], 16 * (m + 1))
                for k in range(2):
                    last = nc.tensor.transpose(bank(0)[:, k * P:(k + 1) * P], f_x[:, u, k, :], ident[:])
                last.then_inc(fxt_ps, 1)

            def experts(q):
                return [pe.value_load(r_expi[0:1, bass.ds(q * 2 + k, 1)], min_val=0, max_val=E - 1) for k in range(2)]

            def first_layer(q, u):
                e = experts(q)
                pe.wait_ge(fxt_done, q + 1)
                for k in range(2):
                    last = nc.tensor.matmul(bank(1 + u)[:, k * HID:(k + 1) * HID], f_xt[:, u, k, :],
                                            w1_sb[:, e[k], :], start=True, stop=True)
                last.then_inc(fh_ps, 1)

            def transpose_hidden(q, u):
                pe.wait_ge(fh_done, 2 * q + 2)
                for k in range(2):
                    for c in range(HC):
                        last = nc.tensor.transpose(bank(3)[:, (k * HC + c) * P:(k * HC + c + 1) * P],
                                                   f_h[:, u, k, c * P:(c + 1) * P], ident[:])
                last.then_inc(fht_ps, 1)

            def second_layer(q, u):
                e = experts(q)
                pe.wait_ge(fht_done, q + 1)
                pe.wait_ge(fy_done, 2 * q + 2)
                for k in range(2):
                    for c in range(HC):
                        last = nc.tensor.matmul(bank(4 + u)[:, k * O:(k + 1) * O], f_ht[:, u, k, c * P:(c + 1) * P],
                                                w2_sb[:, e[k], c, :], start=(c == 0), stop=(c == HC - 1))
                last.then_inc(fy_ps, 1)

            def pair(q, u, m, tokens=True, layer=True, result=True):
                if tokens:
                    transpose_tokens(q + 2, u, m + 1)
                if layer:
                    first_layer(q + 1, 1 - u)
                if result:
                    second_layer(q - 1, 1 - u)
                transpose_hidden(q, u)

            transpose_tokens(0, 0, 0, first=True)
            transpose_tokens(1, 1, 0)
            first_layer(0, 0)
            pair(0, 0, 0, result=False)
            with pe.Fori(0, NPAIR // 2 - 2) as j:
                pair(2 * j + 1, 1, j)
                pair(2 * j + 2, 0, j + 1)
            pair(NPAIR - 3, 1, NPAIR // 2 - 2)
            pair(NPAIR - 2, 0, NPAIR // 2 - 1, tokens=False)
            pair(NPAIR - 1, 1, NPAIR // 2 - 1, tokens=False, layer=False)
            second_layer(NPAIR - 1, 1)


_INS = ["x", "L0_tok_W", "L0_tok_b", "L0_attn_w_qkv", "L0_attn_w_agg", "L0_attn_b_agg",
        "L0_ffn_W1", "L0_ffn_b1", "L0_ffn_W2", "L0_ffn_b2", "L0_ffn_Wg", "L0_ffn_bg"]


def kernel(**inputs):
    import numpy as _np
    import concourse.bacc as _bacc
    from concourse import mybir as _mybir
    from concourse.bass_utils import run_bass_kernel_spmd as _run

    nc = _bacc.Bacc("TRN2", target_bir_lowering=False, num_devices=1)
    arrays, args = {}, []
    for name in _INS:
        a = _np.ascontiguousarray(inputs[name])
        arrays[f"in_{name}"] = a
        args.append(nc.dram_tensor(f"in_{name}", a.shape, _mybir.dt.from_np(a.dtype), kind="ExternalInput").ap())
    batches, steps, width = inputs["x"].shape
    model, taps = inputs["L0_tok_W"].shape
    shape = (batches, steps - taps // width + 1, model)
    out = nc.dram_tensor("out", shape, _mybir.dt.float32, kind="ExternalOutput").ap()
    _program(nc, *args, out)
    return _run(nc, [arrays], core_ids=[0]).results[0]["out"]
```

```python
import struct
from contextlib import ExitStack

import concourse.bass as bass
from concourse import mybir


def _program(nc, x, tok_w, tok_b, w_qkv, w_agg, b_agg, w1, b1, w2, b2, wg, bg, out):
    F32, BF16 = mybir.dt.float32, mybir.dt.bfloat16
    I32, U32 = mybir.dt.int32, mybir.dt.uint32
    ALU, ACT, AX = mybir.AluOpType, mybir.ActivationFunctionType, mybir.AxisListType

    P = 128
    B, T, D = x.shape
    O = tok_w.shape[0]
    CTX = tok_w.shape[1] // D
    L = T - CTX + 1
    H, DH = 8, O // 8
    E, _, HID = w1.shape
    NT = -(-L // P)
    LAST = L - (NT - 1) * P
    LP = NT * P
    HALF = L // 2
    G = 4
    NG = B * H // G
    GB = H // G
    NPART, NPROD = 3, 6
    KR = NPROD * DH
    TT = B * NT
    NSORTS = 2
    HB = B // NSORTS
    HT = HB * NT
    FH = ((HB * L + E * (P - 1)) // P + 1) // 2 * 2
    FT = NSORTS * FH
    NPAIR = FT // 2
    ROW = 2 * O + 1
    HC = HID // P
    EPS = 1e-5
    SCALE = float(DH) ** -0.5
    XLAST = T - (NT - 1) * P
    assert O == P and 2 * D == P and L == 2 * HALF and GB == 2 and NT == 6 and HC == 2 and B == 4 and E % B == 0

    Q_RUNS = [(0, 0, 3), (3, 0, 2), (5, 0, 1)]
    K_RUNS = [(0, 0, 1), (1, 0, 1), (2, 0, 1), (3, 1, 1), (4, 1, 1), (5, 2, 1)]

    parts_dram = nc.dram_tensor("parts_scratch", (2, B, H, NPART * DH, L), BF16).ap()
    xs_dram = nc.dram_tensor("sorted_tokens", (FT * P, ROW), F32).ap()

    ctx = ExitStack()
    with ctx:
        def sb(name, shape, dt=F32):
            return ctx.enter_context(nc.sbuf_tensor(name, shape, dt))

        def sem(name):
            return ctx.enter_context(nc.semaphore(name))

        ps = ctx.enter_context(nc.psum_tensor("ps", [P, 8 * 512], F32))

        def bank(i, n=512):
            return ps[:, i * 512:i * 512 + n]

        qstack = sb("qstack", [P, B * H, L], BF16)
        kstack = sb("kstack", [P, B * H, L], BF16)
        hres = sb("hres", [P, TT, O])
        v_all = sb("v_all", [P, NG, NT, G * DH])
        o_all = sb("o_all", [P, NG, LP])
        ident = sb("ident", [P, P])
        identb = sb("identb", [P, P], BF16)
        w_conv = sb("w_conv", [P, 3 * P])
        w_proj = sb("w_proj", [P, 4 * P])
        tokb_bc = sb("tokb_bc", [P, O])
        bagg_bc = sb("bagg_bc", [P, O])
        stats = sb("stats", [P, NT, 6])
        mv = sb("mv", [P, NT, 2])
        veps = sb("veps", [P, NT])
        nmean = sb("nmean", [P, NT])
        rstd = sb("rstd", [P, NT])
        nmr = sb("nmr", [P, NT])
        veps2, nmean2, rstd2, nmr2 = (sb(n, [P, B, NT]) for n in ("veps2", "nmean2", "rstd2", "nmr2"))
        minus_half = sb("minus_half", [P, NT])
        z = sb("z", [P, NT, O])
        zt = sb("zt", [P, LP])
        x_in = sb("x_in", [P, NT, P])
        xt = sb("xt", [P, LP + 8])
        fill = x_in[:, :, :].rearrange("p t n -> p (t n)")[:, 0:ROW]
        region = sb("region", [P, 4640])
        parts = o_all[:, :, :].rearrange("p g n -> p (g n)")[:, 0:6 * L].bitcast(BF16).rearrange(
            "p (u a c n) -> p u a c n", u=2, a=2, c=NPART)
        rest = region[:, 6 * L // 2:6 * L // 2 + 2 * L].rearrange("p (a n) -> p a n", a=2)
        w_in = region[:, 0:6 * P + 64]
        probs = region[:, 0:12 * HALF].rearrange("p (s n) -> p s n", s=12)
        v_grp = sb("v_grp", [P, NT, G, 32])
        negmax = sb("negmax", [P, 2, 3, G])
        negm = sb("negm", [P, 3, G])
        negr = sb("negr", [P, 3, G])
        mparts = sb("mparts", [P, 2, 3, NPART * G], BF16)
        mrows = sb("mrows", [NPART * G, 2, 3 * P], BF16)
        two_bf16_ones = struct.unpack("<f", struct.pack("<I", 0x3F803F80))[0]
        qf = qstack[:, :, :].rearrange("p a n -> p (a n)").bitcast(F32)
        kf = kstack[:, :, :].rearrange("p a n -> p (a n)").bitcast(F32)
        rows = qf[:, 0:TT * ROW].rearrange("p (t n) -> p t n", t=TT)
        o_bat = kf[:, 0:2 * LP].rearrange("p (g n) -> p g n", g=2)
        w1_sb = kf[:, 1536:1536 + E * HID].rearrange("p (e n) -> p e n", e=E)
        w2_sb = kf[:, 3584:3584 + E * HID].rearrange("p (e c n) -> p e c n", e=E, c=HC)
        b1_bc = kf[:, 5632:5632 + E * HID].rearrange("p (e n) -> p e n", e=E)
        b2_bc = kf[:, 7680:7680 + E * O].rearrange("p (e n) -> p e n", e=E)
        on = kf[:, 8704:8704 + NT * O].rearrange("p (t n) -> p t n", t=NT)
        ont = kf[:, 9472:9472 + LP]
        rden = kf[:, 10240:10240 + NT * H]
        logits = kf[:, 10304:10304 + TT * E].rearrange("p (t e) -> p t e", e=E)
        bg_bc = sb("bg_bc", [P, E])
        wg_sb = sb("wg_sb", [P, E])
        def f_buf(at, n):
            return region[:, at:at + 4 * n].rearrange("p (u k n) -> p u k n", u=2, k=2)

        f_x, f_xt, f_h, f_ht = f_buf(0, O), f_buf(512, P), f_buf(1024, HID), f_buf(2048, HID)
        RING_F = 4
        f_y = region[:, 3072:3072 + RING_F * 2 * O].rearrange("p (u k n) -> p u k n", u=RING_F, k=2)
        f_r = qf[:, (TT + 1) * ROW:(TT + 1) * ROW + RING_F * 2 * (O + 1)].rearrange("p (u k n) -> p u k n", u=RING_F, k=2)
        r_max = sb("r_max", [P, HT])
        r_cand = sb("r_cand", [P, HT, E])
        r_hot = sb("r_hot", [P, HT, E])
        r_e8 = sb("r_e8", [P, E])
        r_valid = sb("r_valid", [P, TT])
        r_scan = sb("r_scan", [P, E, HT])
        r_excl = sb("r_excl", [P, E, HT])
        r_zero = sb("r_zero", [P, E * HT])
        r_cnt = sb("r_cnt", [P, E])
        r_lim = sb("r_lim", [P, HT + 1])
        r_more = sb("r_more", [P, E, HT + 1])
        r_tiles = sb("r_tiles", [P, E])
        r_upto = sb("r_upto", [P, E])
        r_off = sb("r_off", [P, E])
        r_pos = sb("r_pos", [P, HT, E])
        r_posf = sb("r_posf", [P, HT])
        r_posi = sb("r_posi", [P, TT], U32)
        r_tile_no = sb("r_tile_no", [P, FH])
        r_past = sb("r_past", [P, FH, E])
        r_expf = sb("r_expf", [P, FH])
        r_expi = sb("r_expi", [P, FT], I32)
        tri = sb("tri", [P, P])
        ones = sb("ones", [P, P])

        w_loaded, consts, x_pad = sem("w_loaded"), sem("consts"), sem("x_pad")
        w_t_ps, w_t_done = sem("w_t_ps"), sem("w_t_done")
        x_loaded, xt_ps, xt_done, act_warm = sem("x_loaded"), sem("xt_ps"), sem("xt_done"), sem("act_warm")
        conv_ps, h_done = sem("conv_ps"), sem("h_done")
        ln_chain, var_done, rstd_done, z_done = sem("ln_chain"), sem("var_done"), sem("rstd_done"), sem("z_done")
        zt_ps, zt_done = sem("zt_ps"), sem("zt_done")
        q_ps, k_ps, v_ps, v_done = sem("q_ps"), sem("k_ps"), sem("v_ps"), sem("v_done")
        hi_done, rest_done, mid_done, lo_done = sem("hi_done"), sem("rest_done"), sem("mid_done"), sem("lo_done")
        parts_stored, stack_loaded = sem("parts_stored"), sem("stack_loaded")
        batches_stacked = sem("batches_stacked")
        hb_done = sem("hb_done")
        max_ps, max_done, msplit, msplit_chain = sem("max_ps"), sem("max_done"), sem("msplit"), sem("msplit_chain")
        mrow_ps, mrow_done = sem("mrow_ps"), sem("mrow_done")
        mrows_a, mrows_b = sem("mrows_a"), sem("mrows_b")
        score_ps, exp_done, pv_done, vgrp_done, o_done = (
            sem("score_ps"), sem("exp_done"), sem("pv_done"), sem("vgrp_done"), sem("o_done"))
        o_loaded, ot_ps, rden_done, on_done = sem("o_loaded"), sem("ot_ps"), sem("rden_done"), sem("on_done")
        ont_ps, ont_done, agg_ps, h2_done = sem("ont_ps"), sem("ont_done"), sem("agg_ps"), sem("h2_done")
        z2t_ps, z2t_done, log_ps, log_done = sem("z2t_ps"), sem("z2t_done"), sem("log_ps"), sem("log_done")
        ln2_chain, var2_done, rstd2_done, z2_done = sem("ln2_chain"), sem("var2_done"), sem("rstd2_done"), sem("z2_done")
        pow_chain, pow2_chain = sem("pow_chain"), sem("pow2_chain")
        parts_free = sem("parts_free")
        zc_done, wg_loaded, experts_loaded = sem("zc_done"), sem("wg_loaded"), sem("experts_loaded")
        r_chain, r_hot_done, rank_ps, pos_done, expert_done = (
            sem("r_chain"), sem("r_hot_done"), sem("rank_ps"), sem("pos_done"), sem("expert_done"))
        scattered = [sem(f"scattered{i}") for i in range(NSORTS)]
        fxt_ps, fxt_done = sem("fxt_ps"), sem("fxt_done")
        fx_loaded = [sem(f"fx_loaded{u}") for u in range(2)]
        fr_loaded, out_stored = ([sem(f"{n}{u}") for u in range(RING_F)] for n in ("fr_loaded", "out_stored"))
        fh_ps, fh_done, fht_ps, fht_done = sem("fh_ps"), sem("fh_done"), sem("fht_ps"), sem("fht_done")
        fy_ps, fy_done = sem("fy_ps"), sem("fy_done")
        fy_chain = sem("fy_chain")
        turns = sem("turns")
        fill_done, filled, ids_done, o_padded = sem("fill_done"), sem("filled"), sem("ids_done"), sem("o_padded")
        krow_done, krows_done, r_consts = sem("krow_done"), sem("krows_done"), sem("r_consts")

        EXP_FREE, PV_FREE = 3, 3
        ONE_FREE, PARTS_FREE = 1, 2
        FY_FREE = 4
        assert NPAIR % RING_F == 0 and NPAIR > 2 * RING_F and FH // 2 >= RING_F + 3

        UNITS = NT * G
        EARLY = 8
        EARLY_BANKS = {0: (1, None), 1: (0, None), 2: (1, 1), 3: (0, 2), 4: (1, 3), 5: (1, 5), 6: (1, 6), 7: (1, 7),
                       8: (0, None), 9: (1, 8)}
        X_STEP = {1: 7, 0: 17}
        SETS = 2 * NT
        PAIRS = G * SETS
        STACK = 16 * (len(Q_RUNS) + len(K_RUNS))
        HS = NT // 2
        HSTEPS = SETS
        NCONST, IDENT_CONST = 10, 2

        def krows(t):
            return P if t < NT - 1 else LAST

        def unit_banks(s, first=False):
            if first and s in EARLY_BANKS:
                return EARLY_BANKS[s]
            return s % 2, s - 1

        def x_bank(half, first=False):
            return bank(4 if first else 4 + (2 * X_STEP[half] + 1) % 3)

        def experts_from(engine, regs, q, n):
            engine.reg_load(regs[0:n], r_expi[0:1, bass.ds(2 * q, n)])
            e = [engine.snap(reg, min_val=0, max_val=E - 1) for reg in regs[0:n]]
            return [e[k:k + 2] for k in range(0, n, 2)]

        block = ctx.enter_context(nc.Block())

        @block.sync
        def _(sp):
            def load_x(b):
                for k, n in ((0, XLAST), (1, XLAST - 1)):
                    sp.dma_start(x_in[:, 0:NT - 1, k * D:(k + 1) * D],
                                     x[b, k:k + (NT - 1) * P, :].rearrange("(t p) d -> p t d", p=P)).then_inc(x_loaded, 16)
                    sp.dma_start(x_in[0:n, NT - 1, k * D:(k + 1) * D],
                                     x[b, k + (NT - 1) * P:T, :]).then_inc(x_loaded, 16)

            sp.sem_inc(parts_free, PARTS_FREE)
            sp.sem_inc(stack_loaded, ONE_FREE)
            sp.wait_ge(x_pad, 1)
            load_x(0)
            sp.dma_start(w_in[:, 0:CTX * D], tok_w[:, :]).then_inc(w_loaded, 16)
            sp.dma_start(w_in[:, 320:704].rearrange("p (a n) -> p a n", a=3),
                         w_qkv.rearrange("(a p) n -> p a n", p=P)).then_inc(w_loaded, 16)
            sp.dma_start(w_in[:, 704:832], w_agg[:, :]).then_inc(w_loaded, 16)
            sp.dma_start(tokb_bc[:], tok_b.partition_broadcast(P)).then_inc(w_loaded, 16)
            sp.dma_start(bagg_bc[:], b_agg.partition_broadcast(P)).then_inc(w_loaded, 16)
            sp.dma_start(wg_sb[:], wg[:, :]).then_inc(wg_loaded, 16)
            sp.dma_start(bg_bc[:], bg.partition_broadcast(P)).then_inc(wg_loaded, 16)

            def next_x(b):
                sp.wait_ge(xt_ps, b)
                sp.sem_inc(turns, 1)
                load_x(b)

            def store_thirds(b):
                for a in range(2):
                    for c in range(NPART):
                        if c == 0:
                            sp.wait_ge(hi_done, 2 * b + a + 1)
                            sp.sem_inc(turns, 1)
                        elif c == 1:
                            sp.wait_ge(mid_done, 2 * b + a + 1)
                            sp.sem_inc(turns, 1)
                        else:
                            sp.wait_ge(lo_done, 2 * b + a + 1)
                            sp.sem_inc(turns, 1)
                        sp.dma_start(parts_dram[a, b, :, c * DH:(c + 1) * DH, :],
                                     parts[:, bass.ds(b % 2, 1), a, c, :]).then_inc(parts_stored, 16)

            def load_stacks(b):
                sp.wait_ge(parts_stored, 16 * 2 * NPART * (b + 1))
                sp.sem_inc(parts_free, 1)
                sp.wait_ge(stack_loaded, STACK * b + ONE_FREE)
                sp.sem_inc(batches_stacked, 1)
                for a, dst, runs in ((0, qstack, Q_RUNS), (1, kstack, K_RUNS)):
                    for slot, c, n in runs:
                        sp.dma_start(dst[slot * DH:(slot + n) * DH, bass.ds(b * H, H), :],
                                     parts_dram[a, b, :, c * DH:(c + n) * DH, :].rearrange("h r n -> r h n")
                                     ).then_inc(stack_loaded, 16)

            next_x(1)
            sp.wait_ge(krow_done, 1)
            sp.dma_start(kstack[KR:KR + NPART, 1:B * H, :],
                         kstack[KR:KR + NPART, 0:1, :].to_broadcast([NPART, B * H - 1, L])).then_inc(krows_done, 16)
            next_x(2)
            with sp.Fori(0, B - 3) as b:
                next_x(b + 3)
                store_thirds(b)
                load_stacks(b)
            with sp.Fori(B - 3, B - 1) as b:
                store_thirds(b)
                load_stacks(b)
            store_thirds(B - 1)

            def max_rows(half, grp, n_done):
                cols, s = ((0, 3 * P), mrows_a) if half == 0 else ((3 * P, L), mrows_b)
                sp.wait_ge(mrow_done, n_done)
                sp.sem_inc(turns, 1)
                for c in range(NPART):
                    sp.dma_start(qstack[KR + c:KR + c + 1, bass.ds(grp * G, G), cols[0]:cols[1]],
                                 mrows[c * G:(c + 1) * G, half, 0:cols[1] - cols[0]]).then_inc(s, 16)

            def fill_places(i):
                sp.dma_start(xs_dram[bass.ds(i * (FT // NG) * P, FT // NG * P), :].rearrange("(t p) n -> p t n", p=P),
                             fill.rearrange("p (a n) -> p a n", a=1).to_broadcast([P, FT // NG, ROW])).then_inc(filled, 16)

            def load_o(b):
                sp.dma_start(o_bat[:, :, :], o_all[:, bass.ds(b * GB, GB), :]).then_inc(o_loaded, 16)

            EB = E // B

            def load_experts(i):
                e = bass.ds(i * EB, EB)
                sp.dma_start(w1_sb[:, e, :], w1[e, :, :].rearrange("e d n -> d e n")).then_inc(experts_loaded, 16)
                for c in range(HC):
                    sp.dma_start(w2_sb[:, e, c, :], w2[e, c * P:(c + 1) * P, :].rearrange("e p n -> p e n")
                                 ).then_inc(experts_loaded, 16)
                sp.dma_start(b1_bc[:, e, :], b1[e, :].partition_broadcast(P)).then_inc(experts_loaded, 16)
                sp.dma_start(b2_bc[:, e, :], b2[e, :].partition_broadcast(P)).then_inc(experts_loaded, 16)

            max_rows(0, 0, 1)
            load_stacks(B - 1)
            sp.wait_ge(stack_loaded, STACK * B + ONE_FREE)
            sp.sem_inc(batches_stacked, NG)
            sp.wait_ge(fill_done, 2)
            with sp.Fori(0, NG - 1) as g:
                max_rows(1, g, 2 * g + 2)
                max_rows(0, g + 1, 2 * g + 3)
                fill_places(g)
            sp.wait_ge(pv_done, PV_FREE + SETS * (NG - 2))
            sp.wait_ge(o_padded, 1)
            load_o(0)
            sp.wait_ge(ot_ps, 1)
            load_o(1)
            max_rows(1, NG - 1, 2 * NG)
            with sp.Fori(2, B) as b:
                sp.wait_ge(ot_ps, b)
                sp.sem_inc(turns, 1)
                sp.wait_ge(o_done, ONE_FREE + 2 * GB * (b + 1))
                sp.sem_inc(turns, 1)
                load_o(b)
                load_experts(b - 2)
            load_experts(B - 2)
            load_experts(B - 1)
            fill_places(NG - 1)

            def load_pair(q, u, m):
                sp.dma_start(f_x[:, u, :, :], xs_dram[bass.ds(q * 2 * P, 2 * P), 0:O].rearrange("(k p) n -> p k n", p=P)
                             ).then_inc(fx_loaded[u], 16)

            def load_residual(q, u, m, free=True):
                if free:
                    sp.wait_ge(out_stored[u], 32 * m)
                    sp.sem_inc(turns, 1)
                sp.dma_start(f_r[:, u, :, :], xs_dram[bass.ds(q * 2 * P, 2 * P), O:ROW].rearrange("(k p) n -> p k n", p=P)
                             ).then_inc(fr_loaded[u], 16)

            def next_pair(q, u, m):
                sp.wait_ge(fxt_ps, q - 1)
                sp.sem_inc(turns, 1)
                load_pair(q, u, m)

            sp.wait_ge(scattered[0], 16 * HT)
            load_pair(0, 0, 0)
            load_pair(1, 1, 0)
            for u in range(RING_F):
                load_residual(u, u, 0, free=False)
            AHEAD = 3
            for q in range(2, RING_F + AHEAD):
                next_pair(q, q % 2, q // 2)
            sp.wait_ge(scattered[1], 16 * HT)
            with sp.Fori(1, NPAIR // RING_F - 1) as j:
                for u in range(RING_F):
                    next_pair(RING_F * j + u + AHEAD, (u + AHEAD) % 2, RING_F // 2 * j + (u + AHEAD) // 2)
                    load_residual(RING_F * j + u, u, j)
            next_pair(NPAIR - 1, 1, NPAIR // 2 - 1)
            for u in range(RING_F):
                load_residual(NPAIR - RING_F + u, u, NPAIR // RING_F - 1)
            for u in range(RING_F):
                sp.wait_ge(out_stored[u], 32 * (NPAIR // RING_F))

        @block.gpsimd
        def _(pool):
            nc.gpsimd.memset(ident[:], 0.0).then_inc(consts, 1)
            pool.wait_ge(consts, 1)
            nc.gpsimd.affine_select(out=ident[:], in_=ident[:], compare_op=ALU.not_equal, fill=1.0, base=0,
                                    pattern=[[-1, P]], channel_multiplier=1).then_inc(consts, 1)
            nc.gpsimd.memset(xt[:, LP:LP + 8], 0.0).then_inc(consts, 1)
            nc.gpsimd.memset(minus_half[:], -0.5).then_inc(consts, 1)
            nc.gpsimd.memset(ones[:], 1.0).then_inc(consts, 1)
            nc.gpsimd.memset(r_zero[:], 0.0).then_inc(consts, 1)
            nc.gpsimd.memset(v_grp[:], 0.0).then_inc(consts, 1)
            nc.gpsimd.memset(negmax[:], 0.0).then_inc(consts, 1)
            pool.wait_ge(consts, 8)
            nc.gpsimd.tensor_copy(identb[:], ident[:]).then_inc(consts, 1)
            nc.gpsimd.memset(v_grp[:, :, :, DH:DH + 1], 1.0).then_inc(consts, 1)

            def deviations(b, var, chain, done, veps, nmean, rstd, nmr):
                pool.wait_ge(var, b + 1)
                nc.gpsimd.tensor_tensor(rstd, veps, minus_half[:], ALU.pow).then_inc(chain, 1)
                pool.wait_ge(chain, b + 1)
                nc.gpsimd.tensor_tensor(nmr, nmean, rstd, ALU.mult).then_inc(done, 1)

            def residual_bias(b):
                pool.wait_ge(w_loaded, 16 * 5)
                pool.wait_ge(z_done, b + 1)
                h = hres[:, bass.ds(b * NT, NT), :]
                nc.gpsimd.tensor_tensor(h, h, bagg_bc[:].rearrange("p (a n) -> p a n", a=1).to_broadcast([P, NT, O]),
                                        ALU.add).then_inc(hb_done, 1)

            with pool.Fori(0, B) as b:
                deviations(b, var_done, pow_chain, rstd_done, veps[:], nmean[:], rstd[:], nmr[:])
                residual_bias(b)

            nc.gpsimd.iota(r_e8[:], pattern=[[-1, E]], base=E, channel_multiplier=0,
                           allow_small_or_imprecise_dtypes=True).then_inc(r_consts, 1)
            nc.gpsimd.iota(r_lim[:], pattern=[[P, HT + 1]], base=0, channel_multiplier=0,
                           allow_small_or_imprecise_dtypes=True).then_inc(r_consts, 1)
            nc.gpsimd.iota(r_tile_no[:], pattern=[[1, FH]], base=0, channel_multiplier=0,
                           allow_small_or_imprecise_dtypes=True).then_inc(r_consts, 1)
            nc.gpsimd.memset(r_valid[:], 1.0).then_inc(r_consts, 1)
            pool.wait_ge(r_consts, 4)
            nc.gpsimd.affine_select(out=r_valid[:, NT - 1:TT:NT], in_=r_valid[:, NT - 1:TT:NT], compare_op=ALU.is_ge,
                                    fill=0.0, base=LAST - 1, pattern=[[0, B]],
                                    channel_multiplier=-1).then_inc(r_consts, 1)
            nc.gpsimd.affine_select(out=tri[:], in_=ones[:], compare_op=ALU.is_gt, fill=0.0, base=0,
                                    pattern=[[1, P]], channel_multiplier=-1).then_inc(r_consts, 1)

            def split_maxima(half, grp, idx):
                pool.wait_ge(max_done, UNITS * grp + HS * G * (half + 1))
                pool.sem_inc(turns, 1)
                src, dst = negmax[:, half, :, :], mparts[:, half, :, :]
                nc.gpsimd.tensor_copy(dst[:, :, 0:G], src).then_inc(msplit_chain, 1)
                pool.wait_ge(msplit_chain, 3 * idx + 1)
                nc.gpsimd.tensor_tensor(negr[:], src, dst[:, :, 0:G], ALU.subtract).then_inc(msplit_chain, 1)
                pool.wait_ge(msplit_chain, 3 * idx + 2)
                pool.sem_inc(turns, 1)
                nc.gpsimd.tensor_copy(dst[:, :, G:2 * G], negr[:]).then_inc(msplit_chain, 1)
                pool.wait_ge(msplit_chain, 3 * idx + 3)
                nc.gpsimd.tensor_tensor(dst[:, :, 2 * G:3 * G], negr[:], dst[:, :, G:2 * G],
                                        ALU.subtract).then_inc(msplit, 1)

            def copy_values(grp, t):
                nc.gpsimd.tensor_copy(v_grp[:, t, :, 0:DH],
                                      v_all[:, grp, t, :].rearrange("p (h d) -> p h d", h=G)).then_inc(vgrp_done, 1)

            pool.wait_ge(v_done, 1)
            for t in range(NT):
                copy_values(0, t)
            split_maxima(0, 0, 0)
            pool.wait_ge(parts_free, B + PARTS_FREE)
            nc.gpsimd.memset(o_all[:, :, L:LP], 1.0).then_inc(o_padded, 1)

            pool.wait_ge(xt_ps, B)
            nc.gpsimd.memset(fill[:, 0:ROW - 1], 0.0).then_inc(fill_done, 1)
            nc.gpsimd.memset(fill[:, ROW - 1:ROW].bitcast(I32), B * L).then_inc(fill_done, 1)

            split_maxima(1, 0, 1)
            with pool.Fori(0, NG - 1) as g:
                split_maxima(0, g + 1, 2 * g + 2)
                for t in range(NT):
                    if t == NT - 2:
                        split_maxima(1, g + 1, 2 * g + 3)
                    pool.wait_ge(pv_done, SETS * g + PV_FREE + NT + t + 1)
                    pool.sem_inc(turns, 1)
                    copy_values(g + 1, t)

            pool.wait_ge(pv_done, PV_FREE + SETS * (NG - 1))
            nc.gpsimd.iota(rows[:, :, ROW - 1].bitcast(I32), pattern=[[L, B], [P, NT]], base=0,
                           channel_multiplier=1).then_inc(ids_done, 1)

            for b in range(B):
                deviations(b, var2_done, pow2_chain, rstd2_done, *(a[:, b, :] for a in (veps2, nmean2, rstd2, nmr2)))

            pool.wait_ge(ids_done, 1)
            pool.wait_ge(filled, 16 * NG)
            for i in range(NSORTS):
                pool.wait_ge(zc_done, (i + 1) * HB)
                pool.wait_ge(pos_done, i + 1)
                for t in range(i * HT, (i + 1) * HT):
                    n = krows(t % NT)
                    pool.indirect_dma_start(out=xs_dram[:, :],
                                            out_offset=bass.IndirectOffsetOnAxis(ap=r_posi[0:n, t:t + 1], axis=0),
                                            in_=rows[0:n, t, :], in_offset=None).then_inc(scattered[i], 16)
            def scatter_out(q, u):
                for k in range(2):
                    pool.wait_ge(fy_done, FY_FREE + 2 * q + k + 1)
                    pool.sem_inc(turns, 1)
                    pool.indirect_dma_start(out=out.rearrange("b l n -> (b l) n"),
                                            out_offset=bass.IndirectOffsetOnAxis(
                                                ap=f_r[:, u, k, O:O + 1].bitcast(U32), axis=0),
                                            in_=f_y[:, u, k, :], in_offset=None, bounds_check=B * L - 1,
                                            oob_is_err=False).then_inc(out_stored[u], 16)

            with pool.Fori(0, NPAIR // RING_F) as j:
                for u in range(RING_F):
                    scatter_out(RING_F * j + u, u)

        @block.scalar
        def _(act):
            def copy_xt(b):
                act.wait_ge(xt_ps, b + 1)
                nc.scalar.copy(xt[:, 0:LP], ps[:, 0:LP]).then_inc(xt_done, 1)

            def normalise(b, src, ready, done, rstd, nmr):
                act.wait_ge(ready, b + 1)
                for t in range(NT):
                    last = nc.scalar.activation(z[:, t, :], src(b * NT + t), ACT.Identity,
                                                bias=nmr[:, t:t + 1], scale=rstd[:, t:t + 1])
                last.then_inc(done, 1)

            def copy_zt(b):
                act.wait_ge(zt_ps, b + 1)
                nc.scalar.copy(zt[:], ps[:, 4 * 512:4 * 512 + LP]).then_inc(zt_done, 1)

            def qkv_copies(b):
                act.wait_ge(parts_free, b + 1)
                for a, (ready, first) in enumerate(((q_ps, 6), (k_ps, 0))):
                    act.wait_ge(ready, b + 1)
                    nc.scalar.copy(parts[:, bass.ds(b % 2, 1), a, 0, :].rearrange("p u (c n) -> p (u c) n", c=2),
                                   ps[:, first * 512:(first + 2) * 512].rearrange("p (c n) -> p c n", c=2)[:, :, 0:HALF]
                                   ).then_inc(hi_done, 1)
                act.wait_ge(v_ps, b + 1)
                nc.scalar.copy(v_all[:, bass.ds(b * GB, GB), :, :].rearrange("p g t n -> p t g n"),
                               ps[:, 4 * 512:4 * 512 + LP].rearrange("p (t g n) -> p t g n", t=NT, g=GB)
                               ).then_inc(v_done, 1)

            def second_thirds(b):
                for a in range(2):
                    act.wait_ge(rest_done, 2 * b + a + 1)
                    nc.scalar.copy(parts[:, bass.ds(b % 2, 1), a, 1, :], rest[:, a:a + 1, :]).then_inc(mid_done, 1)

            def h_tile(t):
                return hres[:, t, :]

            act.wait_ge(consts, NCONST)
            nc.scalar.copy(nmr[:], minus_half[:]).then_inc(act_warm, 1)
            copy_xt(0)
            act.wait_ge(w_t_ps, 1)
            nc.scalar.copy(w_conv[:, 0:2 * P], bank(2, 2 * P)).then_inc(w_t_done, 1)
            nc.scalar.copy(w_conv[0:D, 2 * P:3 * P], bank(2)[0:D, 2 * P:3 * P]).then_inc(w_t_done, 1)
            nc.scalar.copy(w_proj[:], bank(4)).then_inc(w_t_done, 1)
            copy_xt(1)
            normalise(0, h_tile, rstd_done, z_done, rstd, nmr)
            with act.Fori(0, B - 2) as b:
                copy_zt(b)
                copy_xt(b + 2)
                qkv_copies(b)
                normalise(b + 1, h_tile, rstd_done, z_done, rstd, nmr)
                second_thirds(b)
            copy_zt(B - 2)
            qkv_copies(B - 2)
            normalise(B - 1, h_tile, rstd_done, z_done, rstd, nmr)
            second_thirds(B - 2)
            copy_zt(B - 1)
            qkv_copies(B - 1)
            second_thirds(B - 1)

            act.sem_inc(exp_done, EXP_FREE)
            act.sem_inc(o_done, ONE_FREE)

            def copy_max_rows(half, idx, first=False):
                act.wait_ge(mrow_ps, idx + 1)
                nc.scalar.copy(mrows[:, half, :],
                               x_bank(half, first).bitcast(BF16)[0:NPART * G, 0:HS * P]).then_inc(mrow_done, 1)

            def exponentials(g, s, last=False):
                n = krows((s % HSTEPS) // 2)
                if s == X_STEP[1]:
                    copy_max_rows(1, 2 * g + 1)
                if s == X_STEP[0] and not last:
                    copy_max_rows(0, 2 * g + 2)
                for a in range(2):
                    k = 2 * s + a
                    if k % G == 0:
                        act.wait_ge(pv_done, SETS * g + k // G + 1)
                    act.wait_ge(score_ps, PAIRS * g + k + 1)
                    nc.scalar.activation(probs[0:n, k % 12, :], ps[0:n, (4 + k % 3) * 512:(4 + k % 3) * 512 + HALF],
                                         ACT.Exp, scale=SCALE).then_inc(exp_done, 1)
                if s == HSTEPS + 1:
                    copy_outputs(g, 0)

            def copy_outputs(g, half):
                act.wait_ge(pv_done, SETS * g + PV_FREE + NT * (half + 1))
                nc.scalar.copy(o_all[:, g, half * HALF:(half + 1) * HALF], bank(7, HALF)).then_inc(o_done, 1)

            copy_max_rows(0, 0, first=True)
            act.wait_ge(parts_free, B + PARTS_FREE)
            for s in range(2):
                exponentials(0, s)
            with act.Fori(0, NG - 1) as g:
                for s in range(2, UNITS):
                    exponentials(g, s)
                for s in range(2):
                    exponentials(g + 1, s)
                copy_outputs(g, 1)
            for s in range(2, UNITS):
                exponentials(NG - 1, s, last=True)
            copy_outputs(NG - 1, 1)

            def residual_tile(t):
                return rows[:, t, O:2 * O]

            for b in range(B):
                if b > 0:
                    act.wait_ge(zc_done, b)
                normalise(b, residual_tile, rstd2_done, z2_done, rstd2[:, b, :], nmr2[:, b, :])
                act.wait_ge(z2t_ps, b + 1)
                nc.scalar.copy(zt[:], ps[:, 4 * 512:4 * 512 + LP]).then_inc(z2t_done, 1)

            def copy_tokens(q, u):
                act.wait_ge(fxt_ps, q + 1)
                nc.scalar.copy(f_xt[:, u, :, :], bank(0, 2 * P).rearrange("p (k n) -> p k n", k=2)).then_inc(fxt_done, 1)

            def hidden(q, u):
                act.wait_ge(fht_ps, q + 1)
                nc.scalar.activation(f_ht[:, u, :, :].rearrange("p k n -> p (k n)"), bank(3), ACT.Relu).then_inc(fht_done, 1)

            copy_tokens(0, 0)
            copy_tokens(1, 1)
            copy_tokens(2, 0)
            hidden(0, 0)
            with act.Fori(0, NPAIR // 2 - 2) as j:
                copy_tokens(2 * j + 3, 1)
                hidden(2 * j + 1, 1)
                copy_tokens(2 * j + 4, 0)
                hidden(2 * j + 2, 0)
            copy_tokens(NPAIR - 1, 1)
            for q in range(NPAIR - 3, NPAIR):
                hidden(q, q % 2)

        @block.vector
        def _(dve):
            def ln_stats(b, src, chain, var, veps, nmean):
                dve.sem_inc(turns, 1)
                for t in range(NT):
                    last = nc.vector.bn_stats(stats[:, t, :], src(b * NT + t))
                last.then_inc(chain, 1)
                dve.wait_ge(chain, 2 * b + 1)
                dve.sem_inc(turns, 1)
                for t in range(NT):
                    last = nc.vector.bn_aggr(mv[:, t, :], stats[:, t, :])
                last.then_inc(chain, 1)
                dve.wait_ge(chain, 2 * b + 2)
                nc.vector.tensor_scalar(veps, mv[:, :, 1], EPS, None, ALU.add)
                nc.vector.tensor_scalar(nmean, mv[:, :, 0], -1.0, None, ALU.mult).then_inc(var, 1)

            nc.vector.memset(x_in[:, NT - 1, :], 0.0).then_inc(x_pad, 1)
            def add_conv_bias(b):
                dve.wait_ge(conv_ps, b + 1)
                nc.vector.tensor_tensor(hres[:, bass.ds(b * NT, NT), :],
                                        ps[:, 2 * 512:2 * 512 + LP].rearrange("p (t n) -> p t n", t=NT),
                                        tokb_bc[:].rearrange("p (a n) -> p a n", a=1).to_broadcast([P, NT, O]),
                                        ALU.add).then_inc(h_done, 1)

                dve.wait_ge(h_done, b + 1)
                ln_stats(b, lambda t: hres[:, t, :], ln_chain, var_done, veps[:], nmean[:])

            def rest_of(b, a):
                first = (6, 0)[a]
                dve.wait_ge(hi_done, 2 * b + a + 1)
                nc.vector.tensor_tensor(rest[:, a, :].rearrange("p (c n) -> p c n", c=2),
                                        ps[:, first * 512:(first + 2) * 512].rearrange("p (c n) -> p c n", c=2)[:, :, 0:HALF],
                                        parts[:, bass.ds(b % 2, 1), a, 0, :].rearrange("p u (c n) -> p (u c) n", c=2),
                                        ALU.subtract).then_inc(rest_done, 1)

            def rests(b):
                rest_of(b, 0)
                rest_of(b, 1)

            def last_thirds(b):
                for a in range(2):
                    dve.wait_ge(mid_done, 2 * b + a + 1)
                    nc.vector.tensor_tensor(parts[:, bass.ds(b % 2, 1), a, 2, :], rest[:, a:a + 1, :],
                                            parts[:, bass.ds(b % 2, 1), a, 1, :],
                                            ALU.subtract).then_inc(lo_done, 1)

            def thirds(b):
                rests(b)
                last_thirds(b)

            dve.wait_ge(w_loaded, 16 * 5)
            add_conv_bias(0)
            nc.vector.memset(kf[KR:KR + NPART, 0:HALF], two_bf16_ones).then_inc(krow_done, 1)
            def maxima(grp, units=range(UNITS), first_group=False):
                for s in units:
                    t, h = s // G, s % G
                    first = 2 * unit_banks(s, first_group)[0]
                    n = krows(t)
                    dve.wait_ge(max_ps, UNITS * grp + s + 1)
                    nc.vector.tensor_reduce(negmax[0:n, t // HS, t % HS, h:h + 1],
                                            ps[0:n, first * 512:(first + 2) * 512].rearrange("p (c n) -> p c n", c=2)[:, :, 0:HALF],
                                            axis=AX.XY, op=ALU.max, negate=True).then_inc(max_done, 1)

            with dve.Fori(0, B - 2) as b:
                dve.wait_ge(rstd_done, b + 1)
                add_conv_bias(b + 1)
                thirds(b)
            dve.wait_ge(rstd_done, B - 1)
            add_conv_bias(B - 1)
            rests(B - 2)
            dve.wait_ge(consts, NCONST)
            maxima(0, range(0, 4), True)
            last_thirds(B - 2)
            maxima(0, range(4, 6), True)
            rest_of(B - 1, 0)
            maxima(0, range(6, 7), True)
            rest_of(B - 1, 1)
            maxima(0, range(7, EARLY), True)
            last_thirds(B - 1)

            maxima(0, range(EARLY, UNITS), True)
            with dve.Fori(0, NG - 1) as g:
                maxima(g + 1)

            def normalise(b):
                dve.wait_ge(ot_ps, b + 1)
                heads = ps[:, 0:NT * H * 32].rearrange("p (a n) -> p a n", n=32)
                nc.vector.reciprocal(rden, heads[:, :, DH]).then_inc(rden_done, 1)
                dve.wait_ge(rden_done, b + 1)
                nc.vector.tensor_tensor(on.rearrange("p t (h d) -> p (t h) d", d=DH), heads[:, :, 0:DH],
                                        rden.rearrange("p (a n) -> p a n", n=1).to_broadcast([P, NT * H, DH]),
                                        ALU.mult).then_inc(on_done, 1)

            def copy_ont(b):
                dve.wait_ge(ont_ps, b + 1)
                nc.vector.tensor_copy(ont, ps[:, 0:LP]).then_inc(ont_done, 1)

            def add_residual(b):
                dve.wait_ge(agg_ps, b + 1)
                h = hres[:, bass.ds(b * NT, NT), :]
                nc.vector.tensor_tensor(rows[:, bass.ds(b * NT, NT), O:2 * O], 
                                        ps[:, 2 * 512:2 * 512 + LP].rearrange("p (t n) -> p t n", t=NT), h,
                                        ALU.add).then_inc(h2_done, 1)

            def router_logits(b):
                dve.wait_ge(log_ps, b + 1)
                nc.vector.tensor_tensor(logits[:, bass.ds(b * NT, NT), :],
                                        bank(6 + b % 2, NT * E).rearrange("p (t e) -> p t e", e=E),
                                        bg_bc[:].rearrange("p (a e) -> p a e", a=1).to_broadcast([P, NT, E]),
                                        ALU.add).then_inc(log_done, 1)

            def copy_z(b):
                dve.wait_ge(z2_done, b + 1)
                dve.sem_inc(turns, 1)
                nc.vector.tensor_copy(rows[:, bass.ds(b * NT, NT), 0:O], z[:]).then_inc(zc_done, 1)

            def layer_norm_2(b):
                dve.wait_ge(h2_done, b + 1)
                ln_stats(b, lambda t: rows[:, t, O:2 * O], ln2_chain, var2_done,
                         veps2[:, b, :], nmean2[:, b, :])

            dve.wait_ge(hb_done, B)
            dve.wait_ge(wg_loaded, 16 * 2)
            for b in range(B - 1):
                normalise(b)
                copy_ont(b)
                add_residual(b)
                layer_norm_2(b)
            copy_z(0)
            normalise(3)
            router_logits(0)
            copy_z(1)
            copy_ont(3)
            router_logits(1)

            chain = [0]

            def step(ins):
                chain[0] += 1
                ins.then_inc(r_chain, 1)

            def link(ins):
                step(ins)
                dve.wait_ge(r_chain, chain[0])

            def over_e(ap, n):
                return ap.rearrange("p (n a) -> p n a", a=1).to_broadcast([P, n, E])

            def choose_experts(i):
                tiles = slice(i * HT, (i + 1) * HT)
                dve.wait_ge(log_done, (i + 1) * HB)
                link(nc.vector.tensor_reduce(r_max[:], logits[:, tiles, :], axis=AX.X, op=ALU.max))
                link(nc.vector.tensor_tensor(r_cand[:], logits[:, tiles, :], over_e(r_max[:], HT), ALU.is_equal))
                link(nc.vector.tensor_tensor(r_cand[:], r_cand[:], r_e8[:].rearrange("p (a e) -> p a e", a=1)
                                             .to_broadcast([P, HT, E]), ALU.mult))
                link(nc.vector.tensor_reduce(r_max[:], r_cand[:], axis=AX.X, op=ALU.max))
                link(nc.vector.tensor_tensor(r_hot[:], r_cand[:], over_e(r_max[:], HT), ALU.is_equal))
                nc.vector.tensor_tensor(r_hot[:], r_hot[:], over_e(r_valid[:, tiles], HT), ALU.mult).then_inc(r_hot_done, 1)

            def find_places(i):
                tiles = slice(i * HT, (i + 1) * HT)
                dve.wait_ge(rank_ps, i + 1)
                totals = bank(1, HT * E).rearrange("p (t e) -> p e t", e=E)
                step(nc.vector.tensor_copy(r_excl[:], totals))
                link(nc.vector.tensor_reduce(r_cnt[:], totals, axis=AX.X, op=ALU.add))
                step(nc.vector.tensor_tensor_scan(out=r_scan[:].rearrange("p e t -> p (e t)"), data0=r_zero[:],
                                                  data1=r_excl[:].rearrange("p e t -> p (e t)"), initial=0.0,
                                                  op0=ALU.add, op1=ALU.add))
                link(nc.vector.tensor_tensor(r_more[:], r_cnt[:].rearrange("p (e a) -> p e a", a=1).to_broadcast([P, E, HT + 1]),
                                             r_lim[:].rearrange("p (a n) -> p a n", a=1).to_broadcast([P, E, HT + 1]), ALU.is_gt))
                step(nc.vector.tensor_tensor(r_excl[:], r_scan[:], r_excl[:], ALU.subtract))
                link(nc.vector.tensor_reduce(r_tiles[:], r_more[:], axis=AX.X, op=ALU.add))
                step(nc.vector.tensor_tensor(r_pos[:], bank(0, HT * E).rearrange("p (t e) -> p t e", e=E),
                                             r_excl[:].rearrange("p e t -> p t e"), ALU.add))
                link(nc.vector.tensor_tensor_scan(out=r_upto[:], data0=r_zero[:, 0:E], data1=r_tiles[:], initial=0.0,
                                                  op0=ALU.add, op1=ALU.add))
                link(nc.vector.tensor_tensor(r_off[:], r_upto[:], r_tiles[:], ALU.subtract))
                link(nc.vector.scalar_tensor_tensor(out=r_off[:], in0=r_off[:], scalar=float(P), in1=r_excl[:, :, 0],
                                                    op0=ALU.mult, op1=ALU.subtract))
                link(nc.vector.tensor_tensor(r_pos[:], r_pos[:], r_off[:].rearrange("p (a e) -> p a e", a=1)
                                             .to_broadcast([P, HT, E]), ALU.add))
                link(nc.vector.tensor_tensor(r_pos[:], r_pos[:], r_hot[:], ALU.mult))
                link(nc.vector.tensor_reduce(r_posf[:], r_pos[:], axis=AX.X, op=ALU.add))
                if i > 0:
                    link(nc.vector.tensor_scalar(r_posf[:], r_posf[:], float(i * FH * P), None, ALU.add))
                nc.vector.tensor_copy(r_posi[:, tiles], r_posf[:]).then_inc(pos_done, 1)
                link(nc.vector.tensor_tensor(r_past[:], over_e(r_tile_no[:], FH),
                                             r_upto[:].rearrange("p (a e) -> p a e", a=1).to_broadcast([P, FH, E]), ALU.is_ge))
                link(nc.vector.tensor_reduce(r_expf[:], r_past[:], axis=AX.X, op=ALU.add))
                link(nc.vector.tensor_scalar(r_expf[:], r_expf[:], float(E - 1), None, ALU.min))
                nc.vector.tensor_copy(r_expi[:, i * FH:(i + 1) * FH], r_expf[:]).then_inc(expert_done, 1)

            dve.wait_ge(r_consts, 6)
            choose_experts(0)
            copy_z(2)
            add_residual(3)
            layer_norm_2(3)
            find_places(0)
            router_logits(2)
            copy_z(3)
            router_logits(3)
            choose_experts(1)
            find_places(1)
            dve.wait_ge(expert_done, NSORTS)

            def hidden_bias(q, u, e):
                dve.wait_ge(fh_ps, q + 1)
                for k in range(2):
                    nc.vector.tensor_tensor(f_h[:, u, k, :], bank(1 + u)[:, k * HID:(k + 1) * HID],
                                            b1_bc[:, e[k], :], ALU.add).then_inc(fh_done, 1)

            def results(q, u, m, e):
                dve.wait_ge(fr_loaded[u], 16 * (m + 1))
                for k in range(2):
                    last = nc.vector.tensor_tensor(f_r[:, u, k, 0:O], f_r[:, u, k, 0:O], b2_bc[:, e[k], :], ALU.add)
                last.then_inc(fy_chain, 1)
                dve.wait_ge(fy_chain, q + 1)
                dve.wait_ge(fy_ps, q + 1)
                for k in range(2):
                    nc.vector.tensor_tensor(f_y[:, u, k, :], bank(4 + u % 2)[:, k * O:(k + 1) * O],
                                            f_r[:, u, k, 0:O], ALU.add).then_inc(fy_done, 1)

            dve.wait_ge(experts_loaded, 16 * 5 * B)
            dve.sem_inc(fy_done, FY_FREE)
            expert_regs = [dve.alloc_register(f"dve_expert{i}") for i in range(2 * (RING_F + 2))]
            e = experts_from(dve, expert_regs, 0, 4)
            hidden_bias(0, 0, e[0])
            hidden_bias(1, 1, e[1])
            with dve.Fori(0, NPAIR // RING_F - 1) as j:
                e = experts_from(dve, expert_regs, RING_F * j, 2 * (RING_F + 2))
                for u in range(RING_F):
                    hidden_bias(RING_F * j + u + 2, u % 2, e[u + 2])
                    results(RING_F * j + u, u, j, e[u])
            e = experts_from(dve, expert_regs, NPAIR - RING_F, 2 * RING_F)
            for u in range(RING_F):
                if u + 2 < RING_F:
                    hidden_bias(NPAIR - RING_F + u + 2, u % 2, e[u + 2])
                results(NPAIR - RING_F + u, u, NPAIR // RING_F - 1, e[u])

        @block.tensor
        def _(pe):
            def transpose_weights():
                pe.wait_ge(w_loaded, 16 * 5)
                for c in range(3):
                    w = min(P, CTX * D - c * P)
                    nc.tensor.transpose(bank(2)[0:w, c * P:(c + 1) * P], w_in[:, c * P:c * P + w], ident[:])
                for c in range(4):
                    last = nc.tensor.transpose(bank(4)[:, c * P:(c + 1) * P], w_in[:, 320 + c * P:320 + (c + 1) * P],
                                               ident[:])
                last.then_inc(w_t_ps, 1)
                keep_clock(3, 7)
                pe.wait_ge(w_t_done, 2)

            def transpose_x(b):
                pe.wait_ge(x_loaded, 16 * 4 * (b + 1))
                for t in range(NT):
                    last = nc.tensor.transpose(ps[:, t * P:(t + 1) * P], x_in[:, t, :], ident[:])
                last.then_inc(xt_ps, 1)

            def convolve(b, first=False):
                pe.wait_ge(xt_done, b + 1)
                if not first:
                    pe.wait_ge(h_done, b)
                for t in range(NT):
                    dst = ps[:, 2 * 512 + t * P:2 * 512 + (t + 1) * P]
                    nc.tensor.matmul(dst, xt[:, t * P:(t + 1) * P], w_conv[:, 0:P], start=True, stop=False)
                    nc.tensor.matmul(dst, xt[:, t * P + 2:(t + 1) * P + 2], w_conv[:, P:2 * P], start=False, stop=False)
                    last = nc.tensor.matmul(dst, xt[0:D, t * P + 4:(t + 1) * P + 4], w_conv[0:D, 2 * P:3 * P],
                                            start=False, stop=True)
                last.then_inc(conv_ps, 1)

            def transpose_z(b):
                pe.wait_ge(z_done, b + 1)
                for t in range(NT):
                    last = nc.tensor.transpose(ps[:, 4 * 512 + t * P:4 * 512 + (t + 1) * P], z[:, t, :], ident[:])
                last.then_inc(zt_ps, 1)

            def project_q_or_k(b, a):
                done, first = ((q_ps, 6), (k_ps, 0))[a]
                for c in range(2):
                    last = nc.tensor.matmul(bank(first + c, HALF), w_proj[:, a * P:(a + 1) * P],
                                            zt[:, c * HALF:(c + 1) * HALF], start=True, stop=True)
                last.then_inc(done, 1)

            def project_v(b):
                for t in range(NT):
                    last = nc.tensor.matmul(ps[:, 4 * 512 + t * P:4 * 512 + (t + 1) * P], zt[:, t * P:(t + 1) * P],
                                            w_proj[:, 2 * P:3 * P], start=True, stop=True)
                last.then_inc(v_ps, 1)

            def project(b, b_x):
                pe.wait_ge(zt_done, b + 1)
                project_q_or_k(b, 0)
                pe.wait_ge(xt_done, b_x + 1)
                project_q_or_k(b, 1)
                project_v(b)

            def keep_clock(n, spare):
                for _ in range(n):
                    nc.tensor.matmul(bank(spare, P), ident[:], ident[:], start=True, stop=True)

            pe.wait_ge(consts, IDENT_CONST)
            keep_clock(9, 7)
            pe.wait_ge(consts, NCONST)
            transpose_x(0)
            transpose_weights()
            convolve(0, first=True)
            transpose_x(1)
            convolve(1)
            pe.wait_ge(w_t_done, 3)
            with pe.Fori(0, B - 2) as b:
                keep_clock(4, 5)
                transpose_z(b)
                transpose_x(b + 2)
                project(b, b + 2)
                convolve(b + 2)
                pe.wait_ge(v_done, b + 1)
                pe.wait_ge(rest_done, 2 * b + 2)

            def score_unit(s, grp, first=False):
                t, head = s // G, grp * G + s % G
                pair, before = unit_banks(s, first)
                if before is not None:
                    pe.wait_ge(max_done, UNITS * grp + before)
                n = krows(t)
                for c in range(2):
                    last = nc.tensor.matmul(ps[0:n, (2 * pair + c) * 512:(2 * pair + c) * 512 + HALF],
                                            qstack[0:KR, head, t * P:t * P + n],
                                            kstack[0:KR, head, c * HALF:(c + 1) * HALF], start=True, stop=True)
                last.then_inc(max_ps, 1)

            def transpose_maxima(half, g, first=False):
                pe.wait_ge(msplit, 2 * g + (2 if half else 3))
                if not first:
                    pe.wait_ge(exp_done, PAIRS * g + 2 * X_STEP[half] + 2)
                for t in range(HS):
                    last = nc.tensor.transpose(x_bank(half, first).bitcast(BF16)[0:NPART * G, t * P:(t + 1) * P],
                                               mparts[:, half, t, :], identb[:])
                last.then_inc(mrow_ps, 1)

            def transposed_scores(g, k):
                half, t, head = k // (2 * HSTEPS), k % (2 * HSTEPS) // G, g * G + k % G
                n = krows(t)
                if k == 0:
                    pe.wait_ge(mrows_a, 16 * NPART * (g + 1))
                if k == 2 * HSTEPS:
                    pe.wait_ge(mrows_b, 16 * NPART * (g + 1))
                pe.wait_ge(exp_done, PAIRS * g + k + 1)
                nc.tensor.matmul(ps[0:n, (4 + k % 3) * 512:(4 + k % 3) * 512 + HALF],
                                 kstack[0:KR + NPART, head, t * P:t * P + n],
                                 qstack[0:KR + NPART, head, half * HALF:(half + 1) * HALF],
                                 start=True, stop=True).then_inc(score_ps, 1)

            def value_products(g, n):
                half, t = n // NT, n % NT
                rows = krows(t)
                pe.wait_ge(exp_done, PAIRS * g + G * (n + 1) + EXP_FREE)
                if half == 0:
                    pe.wait_ge(vgrp_done, NT * g + t + 1)
                if t == 0:
                    pe.wait_ge(o_done, 2 * g + half + 1)
                for h in range(G):
                    last = nc.tensor.matmul(ps[32 * h:32 * (h + 1), 7 * 512:7 * 512 + HALF], v_grp[0:rows, t, h, :],
                                            probs[0:rows, (G * n + h) % 12, :], start=(t == 0), stop=(t == NT - 1))
                last.then_inc(pv_done, 1)

            def step(g, s, last=False, before=None):
                transposed_scores(g, 2 * s)
                if s == X_STEP[1]:
                    transpose_maxima(1, g)
                if s == X_STEP[0] and not last:
                    transpose_maxima(0, g)
                if s % 2 == 1 and s > 1:
                    value_products(g, (s - 1) // 2 - 1)
                if s == 1 and before is not None:
                    value_products(before, SETS - 1)
                if s == X_STEP[1]:
                    pe.wait_ge(mrow_done, 2 * g + 2)
                if s == X_STEP[0] and not last:
                    pe.wait_ge(mrow_done, 2 * g + 3)
                transposed_scores(g, 2 * s + 1)

            slot_reg, next_reg = pe.alloc_register("slot"), pe.alloc_register("next_slot")
            pe.sem_inc(pv_done, PV_FREE)
            transpose_z(B - 2)
            project(B - 2, B - 1)
            pe.wait_ge(batches_stacked, 2)
            pe.wait_ge(h_done, B)
            score_unit(0, 0, first=True)
            pe.wait_ge(rest_done, 2 * B - 2)
            for s in range(1, 4):
                score_unit(s, 0, first=True)
            pe.wait_ge(v_done, B - 1)
            transpose_z(B - 1)
            score_unit(4, 0, first=True)
            pe.wait_ge(zt_done, B)
            project_q_or_k(B - 1, 0)
            score_unit(5, 0, first=True)
            project_q_or_k(B - 1, 1)
            score_unit(6, 0, first=True)
            project_v(B - 1)
            score_unit(7, 0, first=True)
            pe.wait_ge(rest_done, 2 * B)
            pe.wait_ge(v_done, B)
            for s in range(EARLY, UNITS - 2):
                score_unit(s, 0, first=True)
                keep_clock(1, 7)
                if s == UNITS - 8:
                    transpose_maxima(0, -1, first=True)
            pe.wait_ge(krow_done, 1)
            pe.wait_ge(krows_done, 16)
            pe.wait_ge(lo_done, 2 * B)
            for s in range(2):
                step(0, s)
                score_unit(UNITS - 2 + s, 0)
            with pe.Fori(0, NG - 1) as g:
                pe.wait_ge(batches_stacked, g + 2)
                for s in range(2, HSTEPS):
                    step(g, s)
                    score_unit(s - 2, g + 1)
                pe.reg_mov(slot_reg, g)
                g_again = pe.snap(slot_reg, min_val=0, max_val=NG - 2)
                for s in range(HSTEPS, UNITS):
                    step(g_again, s)
                    score_unit(s - 2, g_again + 1)
                pe.reg_mov(next_reg, g_again + 1)
                g_next = pe.snap(next_reg, min_val=1, max_val=NG - 1)
                for s in range(2):
                    step(g_next, s, before=g_again)
                    score_unit(UNITS - 2 + s, g_next)

            def transpose_o(b, first=False):
                if not first:
                    pe.wait_ge(h2_done, b)
                pe.wait_ge(o_loaded, 16 * (b + 1))
                for t in range(NT):
                    for g in range(GB):
                        last = nc.tensor.transpose(ps[:, t * 256 + g * P:t * 256 + (g + 1) * P],
                                                   o_bat[:, g, t * P:(t + 1) * P], ident[:])
                last.then_inc(ot_ps, 1)

            def transpose_on(b):
                pe.wait_ge(on_done, b + 1)
                for t in range(NT):
                    last = nc.tensor.transpose(ps[:, t * P:(t + 1) * P], on[:, t, :], ident[:])
                last.then_inc(ont_ps, 1)

            def output_projection(b):
                pe.wait_ge(ont_done, b + 1)
                for t in range(NT):
                    last = nc.tensor.matmul(ps[:, 2 * 512 + t * P:2 * 512 + (t + 1) * P], ont[:, t * P:(t + 1) * P],
                                            w_proj[:, 3 * P:4 * P], start=True, stop=True)
                last.then_inc(agg_ps, 1)

            def transpose_z2(b):
                pe.wait_ge(z2_done, b + 1)
                for t in range(NT):
                    last = nc.tensor.transpose(ps[:, 4 * 512 + t * P:4 * 512 + (t + 1) * P], z[:, t, :], ident[:])
                last.then_inc(z2t_ps, 1)

            def router(b):
                pe.wait_ge(z2t_done, b + 1)
                for t in range(NT):
                    last = nc.tensor.matmul(bank(6 + b % 2)[:, t * E:(t + 1) * E], zt[:, t * P:(t + 1) * P], wg_sb[:],
                                            start=True, stop=True)
                last.then_inc(log_ps, 1)

            C_STEPS = {2: (transpose_o, 0), 4: (transpose_on, 0), 6: (output_projection, 0),
                       8: (transpose_o, 1), 11: (transpose_on, 1), 13: (output_projection, 1),
                       15: (transpose_o, 2), 18: (transpose_on, 2), 20: (output_projection, 2)}
            for s in range(2, UNITS):
                step(NG - 1, s, last=True)
                if s in C_STEPS:
                    part, b = C_STEPS[s]
                    if s == 2:
                        pe.wait_ge(max_done, UNITS * NG)
                        part(b, first=True)
                    else:
                        part(b)
            value_products(NG - 1, SETS - 1)
            pe.wait_ge(o_done, ONE_FREE + 2 * NG)
            pe.wait_ge(h2_done, B - 1)
            keep_clock(6, 3)
            transpose_z2(0)
            transpose_o(3)
            router(0)
            keep_clock(2, 3)
            transpose_z2(1)
            transpose_on(3)
            router(1)
            output_projection(3)

            def rank(i):
                pe.wait_ge(r_hot_done, i + 1)
                hot = r_hot[:].rearrange("p t e -> p (t e)")
                nc.tensor.matmul(bank(0, HT * E), tri[:], hot, start=True, stop=True)
                nc.tensor.matmul(bank(1, HT * E), ones[:], hot, start=True, stop=True).then_inc(rank_ps, 1)

            rank(0)
            transpose_z2(2)
            pe.wait_ge(log_done, 1)
            router(2)
            transpose_z2(3)
            pe.wait_ge(log_done, 2)
            router(3)
            rank(1)
            pe.wait_ge(h2_done, B)
            keep_clock(20, 3)
            pe.wait_ge(expert_done, NSORTS)
            pe.wait_ge(experts_loaded, 16 * 5 * B)

            expert_regs = [pe.alloc_register(f"pe_expert{i}") for i in range(8)]

            def transpose_tokens(q, u, m, first=False):
                if not first:
                    pe.wait_ge(fxt_done, q)
                pe.wait_ge(fx_loaded[u], 16 * (m + 1))
                for k in range(2):
                    last = nc.tensor.transpose(bank(0)[:, k * P:(k + 1) * P], f_x[:, u, k, :], ident[:])
                last.then_inc(fxt_ps, 1)

            def first_layer(q, u, e):
                pe.wait_ge(fxt_done, q + 1)
                for k in range(2):
                    last = nc.tensor.matmul(bank(1 + u)[:, k * HID:(k + 1) * HID], f_xt[:, u, k, :],
                                            w1_sb[:, e[k], :], start=True, stop=True)
                last.then_inc(fh_ps, 1)

            def transpose_hidden(q, u):
                pe.wait_ge(fh_done, 2 * q + 2)
                for k in range(2):
                    for c in range(HC):
                        last = nc.tensor.transpose(bank(3)[:, (k * HC + c) * P:(k * HC + c + 1) * P],
                                                   f_h[:, u, k, c * P:(c + 1) * P], ident[:])
                last.then_inc(fht_ps, 1)

            def second_layer(q, u, e):
                pe.wait_ge(fht_done, q + 1)
                pe.wait_ge(fy_done, 2 * q + 2)
                for k in range(2):
                    for c in range(HC):
                        last = nc.tensor.matmul(bank(4 + u)[:, k * O:(k + 1) * O], f_ht[:, u, k, c * P:(c + 1) * P],
                                                w2_sb[:, e[k], c, :], start=(c == 0), stop=(c == HC - 1))
                last.then_inc(fy_ps, 1)

            def pair(q, u, m, e_next, e_before, tokens=True):
                if tokens:
                    transpose_tokens(q + 2, u, m + 1)
                if e_next is not None:
                    first_layer(q + 1, 1 - u, e_next)
                if e_before is not None:
                    second_layer(q - 1, 1 - u, e_before)
                transpose_hidden(q, u)

            e = experts_from(pe, expert_regs, 0, 4)
            transpose_tokens(0, 0, 0, first=True)
            transpose_tokens(1, 1, 0)
            first_layer(0, 0, e[0])
            pair(0, 0, 0, e[1], None)
            with pe.Fori(0, NPAIR // 2 - 2) as j:
                e = experts_from(pe, expert_regs, 2 * j, 8)
                pair(2 * j + 1, 1, j, e[2], e[0])
                pair(2 * j + 2, 0, j + 1, e[3], e[1])
            e = experts_from(pe, expert_regs, NPAIR - 4, 8)
            pair(NPAIR - 3, 1, NPAIR // 2 - 2, e[2], e[0])
            pair(NPAIR - 2, 0, NPAIR // 2 - 1, e[3], e[1], tokens=False)
            pair(NPAIR - 1, 1, NPAIR // 2 - 1, None, e[2], tokens=False)
            second_layer(NPAIR - 1, 1, e[3])


_INS = ["x", "L0_tok_W", "L0_tok_b", "L0_attn_w_qkv", "L0_attn_w_agg", "L0_attn_b_agg",
        "L0_ffn_W1", "L0_ffn_b1", "L0_ffn_W2", "L0_ffn_b2", "L0_ffn_Wg", "L0_ffn_bg"]


def kernel(**inputs):
    import numpy as _np
    import concourse.bacc as _bacc
    from concourse import mybir as _mybir
    from concourse.bass_utils import run_bass_kernel_spmd as _run

    nc = _bacc.Bacc("TRN2", target_bir_lowering=False, num_devices=1)
    arrays, args = {}, []
    for name in _INS:
        a = _np.ascontiguousarray(inputs[name])
        arrays[f"in_{name}"] = a
        args.append(nc.dram_tensor(f"in_{name}", a.shape, _mybir.dt.from_np(a.dtype), kind="ExternalInput").ap())
    batches, steps, width = inputs["x"].shape
    model, taps = inputs["L0_tok_W"].shape
    shape = (batches, steps - taps // width + 1, model)
    out = nc.dram_tensor("out", shape, _mybir.dt.float32, kind="ExternalOutput").ap()
    _program(nc, *args, out)
    return _run(nc, [arrays], core_ids=[0]).results[0]["out"]
```
